# Optimizing a Trainium2 kernel written in Bass

```python
import numpy as np
import jax
import jax.numpy as jnp

def _softmax(x, axis=-1):
    return jax.nn.softmax(x, axis=axis)

def _gelu(x):
    return jax.nn.gelu(x, approximate=True)

def _silu(x):
    return jax.nn.silu(x)

def _sigmoid(x):
    return jax.nn.sigmoid(x)

def _layernorm(x, axis=-1, eps=1e-05):
    m = jnp.mean(x, axis=axis, keepdims=True)
    v = jnp.var(x, axis=axis, keepdims=True)
    return (x - m) / jnp.sqrt(v + eps)

def _scatter_add(tgt, idx, src, axis=0):
    return tgt.at[idx].add(src)

def _segment_sum(src, seg, n):
    return jax.ops.segment_sum(src, seg, n)
kernel_name = 'mk_xattn_ffn_d1_seqx_r8_beac3e'

def setup_inputs(seed: int=0):
    np.random.seed(seed)
    _w = jnp.asarray

    def _rec_inputs():
        import jax
        import jax.numpy as jnp
        _rk = jax.random.key(seed)
        x = -0.0002928 + 1 * jax.random.normal(jax.random.fold_in(_rk, 1), (32, 128, 128), jnp.float32)
        _lenS = 128 - jax.random.randint(jax.random.fold_in(_rk, 7), (32,), 0, max(1, 128 // 4) + 1, jnp.int32)
        _lenS2 = 128 - jax.random.randint(jax.random.fold_in(_rk, 8), (32,), 0, max(1, 128 // 4) + 1, jnp.int32)
        _ctx_1024P = jax.random.normal(jax.random.fold_in(_rk, 11), (32, 16, 128), jnp.float32)
        _ctx_1024c = jax.random.dirichlet(jax.random.fold_in(_rk, 511), 0.3 * jnp.ones((16,), jnp.float32), (32, 128))
        _ctx_1024t = jnp.einsum('bsk,bkd->bsd', _ctx_1024c, _ctx_1024P)
        _ctx_1024t = _ctx_1024t * jax.lax.rsqrt(jnp.mean(jnp.square(_ctx_1024t)) + 1e-12) * 0.953939
        ctx_1024 = -1.39393e-06 + 0.999914 * (_ctx_1024t + 0.3 * jax.random.normal(jax.random.fold_in(_rk, 611), (32, 128, 128), jnp.float32))
        return (x, ctx_1024)
    x, ctx_1024 = _rec_inputs()

    def _L0_xattn_setup():
        import jax, jax.numpy as jnp
        import numpy as np
        D_MODEL = 128
        NUM_HEADS = 16
        MAX_POS = 1250
        NEG_BIG = 10000000.0

        def rotary(x, max_pos):
            d_half = x.shape[-1] // 2
            freq = jnp.arange(d_half, dtype=x.dtype)
            pos = jnp.arange(x.shape[-2], dtype=x.dtype)
            theta = jnp.asarray(max_pos, x.dtype) ** (-freq / d_half)
            ang = pos[:, None] * theta
            cos, sin = (jnp.cos(ang), jnp.sin(ang))
            xg = x.reshape(*x.shape[:-1], d_half, 2)
            a, b = (xg[..., 0], xg[..., 1])
            ra = a * cos - b * sin
            rb = b * cos + a * sin
            return jnp.stack([ra, rb], axis=-1).reshape(x.shape)
        key = jax.random.key(seed)
        ks = jax.random.split(key, 11)
        B, L, D = (2, 256, D_MODEL)
        s = 1.0 / np.sqrt(D)
        return {'q': jax.random.normal(ks[0], (B, L, D), jnp.float32), 'k': jax.random.normal(ks[1], (B, L, D), jnp.float32), 'v': jax.random.normal(ks[2], (B, L, D), jnp.float32), 'Wq': jax.random.normal(ks[3], (D, D), jnp.float32) * s, 'bq': jnp.zeros((D,), jnp.float32), 'Wk': jax.random.normal(ks[4], (D, D), jnp.float32) * s, 'bk': jnp.zeros((D,), jnp.float32), 'Wv': jax.random.normal(ks[5], (D, D), jnp.float32) * s, 'bv': jnp.zeros((D,), jnp.float32), 'Wo': jax.random.normal(ks[6], (D, D), jnp.float32) * s, 'bo': jnp.zeros((D,), jnp.float32)}
    _L0_xattn_all = _L0_xattn_setup()
    _L0_xattn_in = {k: v for k, v in _L0_xattn_all.items() if k in ('Wq', 'bq', 'Wk', 'bk', 'Wv', 'bv', 'Wo', 'bo')}
    del _L0_xattn_all

    def _L0_ffn_setup():
        import jax, jax.numpy as jnp
        import numpy as np
        HIDDEN = 128
        NUM_EXPERTS = 8
        TOP_K = 2
        B, S = (2, 256)
        key = jax.random.key(seed)
        k1, k2, k3, k4, k5 = jax.random.split(key, 5)
        d, dff, E = (HIDDEN, 4 * HIDDEN, NUM_EXPERTS)
        x = jax.random.normal(k1, (B, S, d), dtype=jnp.float32)
        W1 = jax.random.normal(k2, (E, d, dff), dtype=jnp.float32) * (1.0 / np.sqrt(d))
        b1 = jax.random.normal(k3, (E, dff), dtype=jnp.float32) * 0.01
        W2 = jax.random.normal(k4, (E, dff, d), dtype=jnp.float32) * (1.0 / np.sqrt(dff))
        b2 = jax.random.normal(k5, (E, d), dtype=jnp.float32) * 0.01
        return {'x': x, 'W1': W1, 'b1': b1, 'W2': W2, 'b2': b2}
    _L0_ffn_all = _L0_ffn_setup()
    _L0_ffn_in = {k: v for k, v in _L0_ffn_all.items() if k in ('W1', 'b1', 'W2', 'b2')}
    del _L0_ffn_all
    return {'x': x, 'ctx_1024': ctx_1024, 'L0_xattn_Wq': _L0_xattn_in['Wq'], 'L0_xattn_bq': _L0_xattn_in['bq'], 'L0_xattn_Wk': _L0_xattn_in['Wk'], 'L0_xattn_bk': _L0_xattn_in['bk'], 'L0_xattn_Wv': _L0_xattn_in['Wv'], 'L0_xattn_bv': _L0_xattn_in['bv'], 'L0_xattn_Wo': _L0_xattn_in['Wo'], 'L0_xattn_bo': _L0_xattn_in['bo'], 'L0_ffn_W1': _L0_ffn_in['W1'], 'L0_ffn_b1': _L0_ffn_in['b1'], 'L0_ffn_W2': _L0_ffn_in['W2'], 'L0_ffn_b2': _L0_ffn_in['b2']}

def reference(x, ctx_1024, L0_xattn_Wq, L0_xattn_bq, L0_xattn_Wk, L0_xattn_bk, L0_xattn_Wv, L0_xattn_bv, L0_xattn_Wo, L0_xattn_bo, L0_ffn_W1, L0_ffn_b1, L0_ffn_W2, L0_ffn_b2):
    import jax
    import jax.numpy as jnp

    def _L0_xattn_ref(q, k, v, Wq, bq, Wk, bk, Wv, bv, Wo, bo):
        import jax, jax.numpy as jnp
        import numpy as np
        D_MODEL = 128
        NUM_HEADS = 16
        MAX_POS = 1250
        NEG_BIG = 10000000.0

        def rotary(x, max_pos):
            d_half = x.shape[-1] // 2
            freq = jnp.arange(d_half, dtype=x.dtype)
            pos = jnp.arange(x.shape[-2], dtype=x.dtype)
            theta = jnp.asarray(max_pos, x.dtype) ** (-freq / d_half)
            ang = pos[:, None] * theta
            cos, sin = (jnp.cos(ang), jnp.sin(ang))
            xg = x.reshape(*x.shape[:-1], d_half, 2)
            a, b = (xg[..., 0], xg[..., 1])
            ra = a * cos - b * sin
            rb = b * cos + a * sin
            return jnp.stack([ra, rb], axis=-1).reshape(x.shape)
        B, L, D = q.shape
        H = NUM_HEADS
        dh = D // H
        q = rotary(q @ Wq.T + bq, MAX_POS)
        k = rotary(k @ Wk.T + bk, MAX_POS)
        v = v @ Wv.T + bv
        qh = q.reshape(B, L, H, dh).transpose(0, 2, 1, 3)
        kh = k.reshape(B, L, H, dh).transpose(0, 2, 1, 3)
        vh = v.reshape(B, L, H, dh).transpose(0, 2, 1, 3)
        scores = jnp.einsum('bhqd,bhkd->bhqk', qh, kh) * dh ** (-0.5)
        causal = jnp.triu(jnp.ones((L, L), scores.dtype), 1)
        scores = scores - causal * NEG_BIG
        out = jnp.einsum('bhqk,bhkd->bhqd', jax.nn.softmax(scores, axis=-1), vh)
        out = out.transpose(0, 2, 1, 3).reshape(B, L, D)
        return out @ Wo.T + bo

    def _L0_ffn_ref(x, W1, b1, W2, b2):
        import jax, jax.numpy as jnp
        import numpy as np
        HIDDEN = 128
        NUM_EXPERTS = 8
        TOP_K = 2
        B, S = (2, 256)
        Bm, Sm, d = x.shape
        E = W1.shape[0]
        x_flat = x.reshape(-1, d)
        h = jnp.mod(x_flat[:, :TOP_K].sum(axis=1).astype(jnp.int32), E)
        sel = jnp.stack([h, jnp.mod(h + 1, E)], axis=1)

        def step(acc, params):
            e, W1e, b1e, W2e, b2e = params
            w = jnp.any(sel == e, axis=1).astype(x.dtype) / TOP_K
            y = jnp.maximum(x_flat @ W1e + b1e, 0.0) @ W2e + b2e
            return (acc + w[:, None] * y, None)
        init = jnp.zeros_like(x_flat)
        out_flat, _ = jax.lax.scan(step, init, (jnp.arange(E), W1, b1, W2, b2))
        return out_flat.reshape(Bm, Sm, d)
    x = x + _L0_xattn_ref(_layernorm(x, axis=-1), ctx_1024, ctx_1024, L0_xattn_Wq, L0_xattn_bq, L0_xattn_Wk, L0_xattn_bk, L0_xattn_Wv, L0_xattn_bv, L0_xattn_Wo, L0_xattn_bo)
    x = x + _L0_ffn_ref(_layernorm(x, axis=-1), L0_ffn_W1, L0_ffn_b1, L0_ffn_W2, L0_ffn_b2)
    return x

_drawn_inputs = setup_inputs


def setup_inputs(seed=0):
    import zlib

    import numpy as np

    out = dict(_drawn_inputs(seed))
    spreads = {'L0_xattn_bq': (0.0, 0.1),
     'L0_xattn_bk': (0.0, 0.1),
     'L0_xattn_bv': (0.0, 0.1),
     'L0_xattn_bo': (0.0, 0.1)}
    factors = {'L0_ffn_b1': 8.0, 'L0_ffn_b2': 8.0}
    for name, (base, spread) in spreads.items():
        noise = np.random.default_rng([zlib.crc32(name.encode()), seed]).standard_normal(out[name].shape)
        drawn = base * np.exp(spread * noise) if base else spread * noise
        out[name] = jnp.asarray(drawn.astype(out[name].dtype))
    for name, factor in factors.items():
        out[name] = (out[name] * factor).astype(out[name].dtype)
    return out
```

```python
from contextlib import ExitStack

import numpy as np

import concourse.bass as bass
from concourse import mybir

F32 = mybir.dt.float32
BF16 = mybir.dt.bfloat16
ALU = mybir.AluOpType
ACT = mybir.ActivationFunctionType
AX = mybir.AxisListType

P = 128
B, L, D = 32, 128, 128
H, DH = 16, 8
HP = H // 2
GB = 4
NG = B // GB
GT = GB * L
UNITS = 4
UH = H // UNITS
PARTS = 3
Q_PART = (0, 1, 2, 0, 1, 0)
K_PART = (0, 0, 0, 1, 1, 2)
SLOTS = len(Q_PART)
HROWS = SLOTS * DH
PROWS = 2 * HROWS
MROWS = PROWS + 2
VW = 32
E_N, DFF = 8, 512
FC = DFF // P
EPS = 1e-5
SCALE = DH ** -0.5
BIG = 2.0 ** 15
CYCLE = 2 * GB


def build(nc, a, out):
    with ExitStack() as ctx:
        def sb(name, shape, dt=F32):
            return ctx.enter_context(nc.sbuf_tensor(name, shape, dt))

        def ps(name, shape):
            return ctx.enter_context(nc.psum_tensor(name, shape, F32))

        def sem(name):
            return ctx.enter_context(nc.semaphore(name))

        q_rows = nc.dram_tensor("q_rows", [H, PARTS, DH, GT], BF16, kind="Internal").ap()
        k_rows = nc.dram_tensor("k_rows", [H, SLOTS, DH, GT], BF16, kind="Internal").ap()

        X = sb("X", [P, B, D])
        ctxb = [sb(f"ctxb{i}", [P, GB, D]) for i in range(2)]
        xn = [sb(f"xn{i}", [P, GB, D]) for i in range(2)]
        xT = sb("xT", [P, GT])
        cT = sb("cT", [P, GT])
        rot1 = sb("rot1", [P, GB, L])
        rot2 = sb("rot2", [P, GB, L])
        rot = [sb(f"rot{i}", [P, GT]) for i in "kq"]
        rest = sb("rest", [P, GT])
        parts = [sb(f"parts_{i}", [P, PARTS, GT], BF16) for i in "kq"]
        qst = [sb(f"qst{i}", [P, HP, 2, GT], BF16) for i in range(2)]
        kst = [sb(f"kst{i}", [P, HP, GT], BF16) for i in range(2)]
        vaug = [sb(f"vaug{i}", [P, GB, H, VW]) for i in range(2)]
        ex = [sb(f"ex{i}", [P, H, L]) for i in range(2)]
        oT = sb("oT", [P, UNITS, L])
        attn = [sb(f"attn{i}", [P, H, DH]) for i in range(2)]
        attnT = sb("attnT", [P, L])
        nmax = [sb(f"nmax{i}", [P, H]) for i in range(2)]
        nmh = [sb(f"nmh{i}", [H, 2, L], BF16) for i in range(2)]
        rden = [sb(f"rden{i}", [P, H]) for i in range(2)]
        stats = sb("stats", [P, GB, 6])
        lnb = sb("lnb", [P, 8, GB])
        gate = sb("gate", [P, 2 * CYCLE])
        ident = sb("ident", [P, P])
        bigI = sb("bigI", [P, P], BF16)
        maskr = sb("maskr", [P, UH, L], BF16)
        wk = sb("wk", [P, D])
        wks = sb("wks", [P, D])
        wq = sb("wq", [P, D])
        wqs = sb("wqs", [P, D])
        wv = sb("wv", [P, D])
        wo = sb("wo", [P, D])
        cosT = sb("cosT", [P, L])
        sinT = sb("sinT", [P, L])
        bcol = sb("bcol", [P, 4])
        bvr = sb("bvr", [P, D])
        bor = sb("bor", [P, D])
        w1 = sb("w1", [P, E_N, DFF])
        w2 = sb("w2", [P, E_N, FC, D])
        b1c = sb("b1c", [P, E_N, FC])
        b2r = sb("b2r", [P, E_N, D])
        hid = [ex[0][:, :, :].rearrange("p (c a) l -> p c (a l)", c=FC), ex[1][:, :, :].rearrange("p (c a) l -> p c (a l)", c=FC)]
        acc = sb("acc", [P, GB, D])
        steps_c = sb("steps_c", [P, 34])
        classes = sb("classes", [P, 48])
        rt = sb("rt", [P, GB, 96])
        wt = sb("wt", [P, GB, 3, E_N])

        ps_s = ps("ps_s", [P, 2, UH * L])
        ps_t = ps("ps_t", [P, 2, UH * L])
        ps_o = ps("ps_o", [P, UNITS, L])
        ps_tt = ps("ps_tt", [P, UNITS, P])
        ps_a = ps("ps_a", [P, GT])
        ps_m = ps("ps_m", [P, 512])

        x_in = sem("x_in")
        x_rest_in = sem("x_rest_in")
        ffn_in = sem("ffn_in")
        xb_ready = sem("xb_ready")
        w_in = sem("w_in")
        ctx_in = [sem(f"ctx_in{i}") for i in range(2)]
        consts = sem("consts")
        var_ready = sem("var_ready")
        rstd_ready = sem("rstd_ready")
        ln_op = sem("ln_op")
        xn_ready = sem("xn_ready")
        ctxT_ready = sem("ctxT_ready")
        ctxT_in_sb = sem("ctxT_in_sb")
        xT_ready = sem("xT_ready")
        xT_in_sb = sem("xT_in_sb")
        proj_ready = sem("proj_ready")
        cos_done = sem("cos_done")
        sin_done = sem("sin_done")
        rot_ready = sem("rot_ready")
        part0_ready = sem("part0_ready")
        rest_ready = sem("rest_ready")
        part1_ready = sem("part1_ready")
        part2_ready = sem("part2_ready")
        vproj_ready = sem("vproj_ready")
        v_ready = sem("v_ready")
        k_out = sem("k_out")
        q_out = sem("q_out")
        stacks_in = sem("stacks_in")
        s_ready = sem("s_ready")
        max_done = sem("max_done")
        nmT_ready = sem("nmT_ready")
        nm0_ready = sem("nm0_ready")
        nm_split = sem("nm_split")
        nm_rows = sem("nm_rows")
        st_ready = sem("st_ready")
        exp_done = sem("exp_done")
        mask_done = sem("mask_done")
        pv_done = sem("pv_done")
        oT_in_sb = sem("oT_in_sb")
        o_ready = sem("o_ready")
        rden_ready = sem("rden_ready")
        attn_ready = sem("attn_ready")
        attnT_ready = sem("attnT_ready")
        attnT_in_sb = sem("attnT_in_sb")
        y_ready = sem("y_ready")
        res_done = sem("res_done")
        h_even = sem("h_even")
        h_odd = sem("h_odd")
        relu_even = sem("relu_even")
        relu_odd = sem("relu_odd")
        ffn_y_ready = sem("ffn_y_ready")
        route_op = sem("route_op")
        b2_done = sem("b2_done")
        acc_done = sem("acc_done")
        out_stored = sem("out_stored")

        block = ctx.enter_context(nc.Block())

        def run_steps(eng, step):
            step(0, 0)
            whole = (B - 1) // CYCLE
            with eng.Fori(0, whole) as c:
                for k in range(1, CYCLE + 1):
                    step(c * CYCLE + k, k % CYCLE)
            for n in range(whole * CYCLE + 1, B):
                step(n, n % CYCLE)

        def known(n):
            return isinstance(n, int)

        def group_after(n, k):
            g = n // GB + 1 if known(n) else (n - k % GB) // GB + 1
            return None if known(n) and g >= NG else g

        @block.sync
        def _(sp):
            xv = a["x"].rearrange("b l d -> l b d")
            cv = a["ctx_1024"].rearrange("b l d -> l b d")

            def load_ctx(g, par):
                sp.dma_start(ctxb[par][:], cv[:, bass.ts(g, GB), :]).then_inc(ctx_in[par], 16)

            sp.dma_start(ident[:], a["ident"]).then_inc(w_in, 16)
            load_ctx(0, 0)
            sp.dma_start(X[:, 0:GB, :], xv[:, 0:GB, :]).then_inc(x_in, 16)
            for t, n in ((wk, "WkT"), (wks, "WksT"), (wq, "WqT"), (wqs, "WqsT"), (wv, "WvT"), (wo, "WoT"),
                         (cosT, "cosT"), (sinT, "sinT"), (bcol, "bcol"), (bigI, "bigI"), (maskr, "maskr")):
                sp.dma_start(t[:], a[n]).then_inc(w_in, 16)
            sp.dma_start(bvr[:], a["L0_xattn_bv"].rearrange("(a d) -> a d", a=1).to_broadcast((P, D))).then_inc(w_in, 16)
            sp.dma_start(bor[:], a["L0_xattn_bo"].rearrange("(a d) -> a d", a=1).to_broadcast((P, D))).then_inc(w_in, 16)
            sp.dma_start(steps_c[:], a["steps"].to_broadcast((P, 34))).then_inc(w_in, 16)
            sp.dma_start(classes[:], a["classes"].to_broadcast((P, 48))).then_inc(w_in, 16)
            load_ctx(1, 1)
            for g in range(1, NG):
                sp.dma_start(X[:, bass.ts(g, GB), :], xv[:, bass.ts(g, GB), :]).then_inc(x_rest_in, 16)
            sp.dma_start(w1[:], a["L0_ffn_W1"].rearrange("e d f -> d e f")).then_inc(ffn_in, 16)
            sp.dma_start(w2[:], a["L0_ffn_W2"].rearrange("e (c p) d -> p e c d", p=P)).then_inc(ffn_in, 16)
            sp.dma_start(b1c[:], a["b1c"]).then_inc(ffn_in, 16)
            sp.dma_start(b2r[:], a["L0_ffn_b2"].rearrange("(a e) d -> a e d", a=1).to_broadcast((P, E_N, D))).then_inc(ffn_in, 16)

            def k_stack(g, par):
                if not (known(g) and g == 0):
                    sp.wait_ge(stacks_in, 16 * 8 * g)
                sp.wait_ge(part2_ready, 2 * g + 1)
                for s in range(SLOTS):
                    sp.dma_start(k_rows[:, s], parts[0][:, K_PART[s], :]).then_inc(k_out, 16)
                sp.wait_ge(k_out, 16 * SLOTS * (g + 1))
                for m in range(2):
                    sp.dma_start(kst[par][m * HROWS:(m + 1) * HROWS, :, :],
                                 k_rows.rearrange("(g m) s r t -> m (s r) g t", m=2)[m]).then_inc(stacks_in, 16)

            def q_stack(g, par):
                sp.wait_ge(part2_ready, 2 * g + 2)
                for s in range(PARTS):
                    sp.dma_start(q_rows[:, s], parts[1][:, s, :]).then_inc(q_out, 16)
                sp.wait_ge(q_out, 16 * PARTS * (g + 1))
                for m in range(2):
                    qv = q_rows.rearrange("(g m) s r t -> m (s r) g t", m=2)[m]
                    at = m * HROWS
                    for w in (PARTS, 2, 1):
                        sp.dma_start(qst[par][at:at + w * DH, :, m, :], qv[0:w * DH]).then_inc(stacks_in, 16)
                        at += w * DH

            def maxima_rows(m, k):
                sp.wait_ge(nm_split, m + 1)
                b = k % GB
                for s in range(2):
                    sp.dma_start(qst[k // GB][PROWS + s:PROWS + s + 1, :, :, b * L:(b + 1) * L],
                                 nmh[k % 2][:, s, :]).then_inc(nm_rows, 16)

            sp.wait_ge(consts, 6)
            k_stack(0, 0)
            q_stack(0, 0)
            maxima_rows(0, 0)

            def step(n, k):
                g = group_after(n, k)
                par = (k // GB + 1) % 2
                b = k % GB
                if g is not None and b == 1:
                    k_stack(g, par)
                if not (known(n) and n == B - 1):
                    maxima_rows(n + 1, (k + 1) % CYCLE)
                if g is not None and b == 2:
                    q_stack(g, par)
                    if not (known(g) and g + 1 >= NG):
                        sp.wait_ge(ctxT_ready, g)
                        load_ctx(g + 1, 1 - par)

            run_steps(sp, step)

            ov = out.rearrange("b l d -> l b d")
            sp.sem_inc(out_stored, 16)
            with sp.Fori(0, NG) as g:
                sp.wait_ge(acc_done, E_N * g + E_N + 2)
                sp.dma_start(ov[:, bass.ts(g, GB), :], acc[:]).then_inc(out_stored, 16)
            sp.wait_ge(out_stored, 16 * (NG + 1))

        @block.gpsimd
        def _(pool):
            for i in range(2):
                nc.gpsimd.memset(qst[i][:], 0.0).then_inc(consts, 1)
            for i in range(2):
                nc.gpsimd.memset(kst[i][:], 1.0).then_inc(consts, 1)
            for i in range(2):
                nc.gpsimd.memset(vaug[i][:], 0.0).then_inc(consts, 1)
            pool.wait_ge(consts, 6)
            for i in range(2):
                nc.gpsimd.memset(vaug[i][:, :, :, DH:DH + 1], 1.0).then_inc(consts, 1)
            nc.gpsimd.memset(lnb[:, 7, :], -0.5).then_inc(consts, 1)
            nc.gpsimd.memset(gate[:], 0.0).then_inc(consts, 1)
            pool.wait_ge(consts, 10)

            def rstd(g):
                pool.wait_ge(var_ready, g + 1)
                nc.gpsimd.tensor_tensor(lnb[:, 6, :], lnb[:, 5, :], lnb[:, 7, :], ALU.pow).then_inc(rstd_ready, 1)

            def split(g, i):
                pool.wait_ge(sin_done, 2 * g + i + 1)
                nc.gpsimd.tensor_tensor(rot[i][:], rot1[:].rearrange("p b l -> p (b l)"),
                                        rot2[:].rearrange("p b l -> p (b l)"), ALU.add).then_inc(rot_ready, 1)
                pool.wait_ge(part0_ready, 2 * g + i + 1)
                nc.gpsimd.tensor_tensor(rest[:], rot[i][:], parts[i][:, 0, :], ALU.subtract).then_inc(rest_ready, 1)
                pool.wait_ge(part1_ready, 2 * g + i + 1)
                nc.gpsimd.tensor_tensor(parts[i][:, 2, :], rest[:], parts[i][:, 1, :],
                                        ALU.subtract).then_inc(part2_ready, 1)

            def mask(n, k, u):
                pool.wait_ge(exp_done, UNITS * n + u + 1)
                j = (k * UNITS + u) % (2 * CYCLE)
                nc.gpsimd.tensor_tensor(gate[:, j:j + 1], lnb[:, 7, 0:1], lnb[:, 7, 0:1], ALU.add)
                e = ex[k % 2][:, u * UH:(u + 1) * UH, :]
                nc.gpsimd.affine_select(out=e, in_=e, pattern=[[0, UH], [1, L]], compare_op=ALU.is_ge, fill=0.0,
                                        base=0, channel_multiplier=-1).then_inc(mask_done, 1)

            rstd(0)
            split(0, 0)
            split(0, 1)

            def step(n, k):
                g = group_after(n, k)
                b = k % GB
                for u in range(UNITS):
                    mask(n, k, u)
                    if g is not None and b == 0 and u == 3:
                        split(g, 0)
                        rstd(g)
                    if g is not None and b == 1 and u == 3:
                        split(g, 1)

            run_steps(pool, step)
            with pool.Fori(NG, 2 * NG) as g:
                rstd(g)

        @block.scalar
        def _(act):
            def evac_ctxT(g):
                act.wait_ge(ctxT_ready, g + 1)
                nc.scalar.activation(cT[:], ps_a[:], ACT.Copy).then_inc(ctxT_in_sb, 1)

            def evac_xT(g):
                act.wait_ge(xT_ready, g + 1)
                nc.scalar.activation(xT[:], ps_a[:], ACT.Copy).then_inc(xT_in_sb, 1)

            def split(g, i):
                if not (known(g) and g == 0):
                    act.wait_ge((k_out, q_out)[i], 16 * (SLOTS, PARTS)[i] * g)
                act.wait_ge(rot_ready, 2 * g + i + 1)
                nc.scalar.activation(parts[i][:, 0, :], rot[i][:], ACT.Copy).then_inc(part0_ready, 1)
                act.wait_ge(rest_ready, 2 * g + i + 1)
                nc.scalar.activation(parts[i][:, 1, :], rest[:], ACT.Copy).then_inc(part1_ready, 1)

            def exp(n, k, u):
                if u == 0 and not (known(n) and n == 0):
                    act.wait_ge(pv_done, n)
                act.wait_ge(st_ready, UNITS * n + u + 1)
                nc.scalar.activation(ex[k % 2][:, u * UH:(u + 1) * UH, :],
                                     ps_t[:, u % 2, :].rearrange("p (h l) -> p h l", h=UH),
                                     ACT.Exp, scale=SCALE).then_inc(exp_done, 1)

            def evac_o(n):
                act.wait_ge(pv_done, n + 2)
                nc.scalar.activation(oT[:], ps_o[:], ACT.Copy).then_inc(oT_in_sb, 1)

            def evac_attnT(t):
                act.wait_ge(attnT_ready, t + 1)
                nc.scalar.activation(attnT[:], ps_m[:, 128:256], ACT.Copy).then_inc(attnT_in_sb, 1)

            evac_ctxT(0)
            evac_xT(0)
            split(0, 0)
            split(0, 1)

            def step(n, k):
                g = group_after(n, k)
                b = k % GB
                if g is not None and b == 0:
                    evac_ctxT(g)
                if g is not None and b == 1:
                    evac_xT(g)
                exp(n, k, 0)
                exp(n, k, 1)
                if not (known(n) and n == 0):
                    evac_attnT(n - 1)
                exp(n, k, 2)
                exp(n, k, 3)
                evac_o(n)
                if g is not None and b < 2:
                    split(g, b)

            run_steps(act, step)
            evac_attnT(B - 1)

            act.wait_ge(ffn_in, 64)
            act.wait_ge(y_ready, B)
            act.sem_inc(relu_even, 1)
            with act.Fori(0, NG) as g:
                evac_xT(g + NG)
                for e in range(E_N):
                    act.wait_ge(ffn_y_ready, E_N * g + e + 1)
                    for c in range(0, FC, 2):
                        act.wait_ge(h_even, 16 * g + 2 * e + c // 2 + 1)
                        nc.scalar.activation(hid[e % 2][:, c, :], ps_s[:, c % 2, :], ACT.Relu,
                                             bias=b1c[:, e, c:c + 1]).then_inc(relu_even, 1)

        @block.tensor
        def _(pe):
            mm, tr = nc.tensor.matmul, nc.tensor.transpose
            pe.sem_inc(pv_done, 1)

            def ctx_transpose(g, par):
                pe.wait_ge(ctx_in[par], 8 * (g - par) + 16)
                if not (known(g) and g == 0):
                    pe.wait_ge(v_ready, g)
                for t in range(GB):
                    i = tr(ps_a[:, t * L:(t + 1) * L], ctxb[par][:, t, :], ident[:])
                i.then_inc(ctxT_ready, 1)

            def x_transpose(g, par):
                pe.wait_ge(xn_ready, GB * (g + 1))
                pe.wait_ge(sin_done, 2 * g + 1)
                for t in range(GB):
                    i = tr(ps_a[:, t * L:(t + 1) * L], xn[par][:, t, :], ident[:])
                i.then_inc(xT_ready, 1)

            def project(g, i):
                pe.wait_ge((ctxT_in_sb, cos_done, xT_in_sb, cos_done)[i], (g + 1, 2 * g + 1, g + 1, 2 * g + 2)[i])
                mm(ps_a[:], (wk, wks, wq, wqs)[i][:], (cT, cT, xT, xT)[i][:], start=True, stop=True).then_inc(proj_ready, 1)

            def project_v(g):
                pe.wait_ge(sin_done, 2 * g + 2)
                for t in range(GB):
                    i = mm(ps_a[:, t * L:(t + 1) * L], cT[:, t * L:(t + 1) * L], wv[:], start=True, stop=True)
                i.then_inc(vproj_ready, 1)

            def scores(m, k):
                b, par = k % GB, k // GB
                tok = slice(b * L, (b + 1) * L)
                for u in range(UNITS):
                    if u == 0 and b == 0:
                        pe.wait_ge(stacks_in, 16 * 8 * (m // GB + 1) if known(m) else 32 * (m + GB))
                    if not (known(m) and m * UNITS + u < 2):
                        pe.wait_ge(max_done, UNITS * m + u - 1)
                    bank = ps_s[:, u % 2, :]
                    mm(bank, bigI[:], maskr[:].rearrange("p h l -> p (h l)"), start=True, stop=False, skip_group_check=True)
                    for j in range(UH):
                        h = u * UH + j
                        i = mm(bank[:, j * L:(j + 1) * L], qst[par][0:PROWS, h // 2, h % 2, tok],
                               kst[par][0:PROWS, h // 2, tok], start=False, stop=(j == UH - 1), skip_group_check=True)
                    i.then_inc(s_ready, 1)

            def maxima_transpose(m, k):
                pe.wait_ge(max_done, UNITS * (m + 1))
                if not (known(m) and m == 0):
                    pe.wait_ge(nm_split, m)
                if not (known(m) and m < 2):
                    pe.wait_ge(res_done, m - 1)
                tr(ps_m[0:H, 0:L], nmax[k % 2][:], ident[:]).then_inc(nmT_ready, 1)

            def scores_t(n, k, u):
                b, par = k % GB, k // GB
                tok = slice(b * L, (b + 1) * L)
                if u == 0:
                    pe.wait_ge(nm_rows, 32 * (n + 1))
                if not (known(n) and n * UNITS + u < 2):
                    pe.wait_ge(exp_done, UNITS * n + u - 1)
                for j in range(2):
                    g = 2 * u + j
                    i = mm(ps_t[:, u % 2, j * 2 * L:(j + 1) * 2 * L], kst[par][0:MROWS, g, tok],
                           qst[par][0:MROWS, g, :, tok], start=True, stop=True)
                i.then_inc(st_ready, 1)

            def weigh_v(n, k, u):
                b, par = k % GB, k // GB
                if u == 0:
                    pe.wait_ge(v_ready, n // GB + 1 if known(n) else (n - b) // GB + 1)
                    if not (known(n) and n == 0):
                        pe.wait_ge(oT_in_sb, n)
                pe.wait_ge(mask_done, UNITS * n + u + 1)
                for j in range(UH):
                    h = u * UH + j
                    i = mm(ps_o[j * VW:(j + 1) * VW, u, :], vaug[par][:, b, h, :], ex[k % 2][:, h, :], start=True, stop=True)
                if u == UNITS - 1:
                    i.then_inc(pv_done, 1)

            def o_transpose(t):
                pe.wait_ge(oT_in_sb, t + 1)
                if not (known(t) and t == 0):
                    pe.wait_ge(attn_ready, t + 1)
                for u in range(UNITS):
                    i = tr(ps_tt[:, u, :], oT[:, u, :], ident[:])
                i.then_inc(o_ready, 1)

            def attn_transpose(t, k):
                pe.wait_ge(attn_ready, t + 2)
                if known(t) and t + 2 >= B:
                    pe.wait_ge(res_done, t + 1)
                else:
                    pe.wait_ge(nm_split, t + 3)
                tr(ps_m[:, 128:256], attn[k % 2][:].rearrange("p h d -> p (h d)"), ident[:]).then_inc(attnT_ready, 1)

            def project_o(t):
                pe.wait_ge(attnT_in_sb, t + 2)
                mm(ps_m[:, 256:384], attnT[:], wo[:], start=True, stop=True).then_inc(y_ready, 1)

            pe.wait_ge(w_in, 16 * 16)
            ctx_transpose(0, 0)
            project(0, 0)
            project(0, 1)
            x_transpose(0, 0)
            project(0, 2)
            project(0, 3)
            project_v(0)
            pe.wait_ge(consts, 10)
            scores(0, 0)
            maxima_transpose(0, 0)

            def step(n, k):
                g = group_after(n, k)
                par = (k // GB + 1) % 2
                b = k % GB
                more = not (known(n) and n == B - 1)
                tail = not (known(n) and n == 0)
                stage_a = [] if g is None else {
                    0: [lambda: ctx_transpose(g, par), lambda: project(g, 0), lambda: project(g, 1), None],
                    1: [lambda: x_transpose(g, par), lambda: project(g, 2), lambda: project(g, 3),
                        lambda: project_v(g)]}.get(b, [])

                def a_piece(i):
                    if i < len(stage_a) and stage_a[i]:
                        stage_a[i]()

                if more:
                    scores(n + 1, (k + 1) % CYCLE)
                a_piece(0)
                if tail:
                    o_transpose(n - 1)
                scores_t(n, k, 0)
                scores_t(n, k, 1)
                if more:
                    maxima_transpose(n + 1, (k + 1) % CYCLE)
                weigh_v(n, k, 0)
                a_piece(1)
                if tail:
                    attn_transpose(n - 1, (k - 1) % CYCLE)
                scores_t(n, k, 2)
                weigh_v(n, k, 1)
                a_piece(2)
                scores_t(n, k, 3)
                if tail:
                    project_o(n - 1)
                weigh_v(n, k, 2)
                a_piece(3)
                weigh_v(n, k, 3)

            run_steps(pe, step)
            o_transpose(B - 1)
            attn_transpose(B - 1, CYCLE - 1)
            project_o(B - 1)

            pe.wait_ge(ffn_in, 64)
            pe.sem_inc(ffn_y_ready, 2)
            with pe.Fori(0, NG) as g:
                pe.wait_ge(xn_ready, GB * (g + NG + 1))
                pe.wait_ge(xT_in_sb, g + NG)
                for t in range(GB):
                    i = tr(ps_a[:, t * L:(t + 1) * L], xn[0][:, t, :], ident[:])
                i.then_inc(xT_ready, 1)
                pe.wait_ge(xT_in_sb, g + NG + 1)

                def up(e, c):
                    idx = 16 * g + 2 * e + c // 2
                    pe.wait_ge((relu_even, relu_odd)[c % 2], idx + 1)
                    mm(ps_s[:, c % 2, :], w1[:, e, c * P:(c + 1) * P], xT[:], start=True,
                       stop=True).then_inc((h_even, h_odd)[c % 2], 1)

                def down(e, c):
                    if c == 0:
                        pe.wait_ge(acc_done, E_N * g + e + 1)
                    pe.wait_ge((relu_even, relu_odd)[c % 2], 16 * g + 2 * e + c // 2 + 2)
                    for t in range(GB):
                        i = mm(ps_t[:, e % 2, t * D:(t + 1) * D], hid[e % 2][:, c, t * L:(t + 1) * L], w2[:, e, c, :],
                               start=(c == 0 and t == 0), stop=(c == FC - 1), skip_group_check=True)
                    if c == FC - 1:
                        i.then_inc(ffn_y_ready, 1)

                units = [(e, c) for e in range(E_N) for c in range(FC)]
                up(*units[0])
                for j, (e, c) in enumerate(units):
                    if j + 1 < len(units):
                        up(*units[j + 1])
                    down(e, c)

        @block.vector
        def _(dve):
            tt, ts = nc.vector.tensor_tensor, nc.vector.tensor_scalar
            dve.sem_inc(attn_ready, 1)
            dve.sem_inc(res_done, 1)
            dve.sem_inc(attnT_in_sb, 1)

            LN_OPS = 12

            def layernorm(g, dst, x_at, ready, base):
                for t in range(GB):
                    nc.vector.bn_stats(stats[:, t, :], x_at(t)).then_inc(ln_op, 1)
                dve.wait_ge(ln_op, base + 4)
                tt(lnb[:, 0, :], stats[:, :, 1], stats[:, :, 4], ALU.add).then_inc(ln_op, 1)
                tt(lnb[:, 1, :], stats[:, :, 1], stats[:, :, 4], ALU.subtract).then_inc(ln_op, 1)
                tt(lnb[:, 2, :], stats[:, :, 2], stats[:, :, 5], ALU.add).then_inc(ln_op, 1)
                dve.wait_ge(ln_op, base + 7)
                ts(lnb[:, 0, :], lnb[:, 0, :], 0.5, None, ALU.mult).then_inc(ln_op, 1)
                tt(lnb[:, 3, :], lnb[:, 1, :], lnb[:, 1, :], ALU.mult).then_inc(ln_op, 1)
                ts(lnb[:, 4, :], lnb[:, 2, :], 1.0 / D, EPS, ALU.mult, ALU.add).then_inc(ln_op, 1)
                dve.wait_ge(ln_op, base + 10)
                nc.vector.scalar_tensor_tensor(lnb[:, 5, :], lnb[:, 3, :], 0.25, lnb[:, 4, :], ALU.mult,
                                               ALU.add).then_inc(var_ready, 1)
                dve.wait_ge(rstd_ready, ready)
                for t in range(GB):
                    ts(dst[:, t, :], x_at(t), lnb[:, 0, t:t + 1], lnb[:, 6, t:t + 1], ALU.subtract,
                       ALU.mult).then_inc(xn_ready, 1)

            def norm_x(g, par):
                dve.wait_ge(*((x_in, 16) if known(g) and g == 0 else (x_rest_in, 16 * (NG - 1))))
                layernorm(g, xn[par], lambda t: X[:, g * GB + t, :], g + 1, 10 * g)
                dve.wait_ge(xn_ready, GB * (g + 1))
                for t in range(GB):
                    tt(X[:, g * GB + t, :], X[:, g * GB + t, :], bor[:], ALU.add).then_inc(xb_ready, 1)

            def rotate(g, i, half):
                dve.wait_ge(proj_ready, 4 * g + 2 * i + half + 1)
                if half == 0 and not (known(g) and g == 0 and i == 0):
                    dve.wait_ge(rot_ready, 2 * g + i)
                dst, tab, done = ((rot1, cosT, cos_done), (rot2, sinT, sin_done))[half]
                nc.vector.scalar_tensor_tensor(dst[:], ps_a[:].rearrange("p (b l) -> p b l", b=GB),
                                               bcol[:, 2 * i + half:2 * i + half + 1],
                                               tab[:].rearrange("p (b l) -> p b l", b=1).to_broadcast((P, GB, L)),
                                               ALU.add, ALU.mult).then_inc(done, 1)

            def keep_v(g, par):
                dve.wait_ge(vproj_ready, g + 1)
                if not (known(g) and g < 2):
                    dve.wait_ge(pv_done, GB * (g - 1) + 1)
                tt(vaug[par][:, :, :, 0:DH], ps_a[:].rearrange("p (b h d) -> p b h d", b=GB, h=H),
                   bvr[:].rearrange("p (b h d) -> p b h d", b=1, h=H).to_broadcast((P, GB, H, DH)),
                   ALU.add).then_inc(v_ready, 1)

            def maxima(m, k):
                for u in range(UNITS):
                    dve.wait_ge(s_ready, UNITS * m + u + 1)
                    nc.vector.tensor_reduce(nmax[k % 2][:, u * UH:(u + 1) * UH],
                                            ps_s[:, u % 2, :].rearrange("p (h l) -> p h l", h=UH),
                                            AX.X, ALU.max, negate=True).then_inc(max_done, 1)

            def split_maxima(m, k):
                dve.wait_ge(nmT_ready, m + 1)
                if not (known(m) and m < 2):
                    dve.wait_ge(nm_rows, 32 * (m - 1))
                nc.vector.tensor_copy(nmh[k % 2][:, 0, :], ps_m[0:H, 0:L]).then_inc(nm0_ready, 1)
                dve.wait_ge(nm0_ready, m + 1)
                tt(nmh[k % 2][:, 1, :], ps_m[0:H, 0:L], nmh[k % 2][:, 0, :], ALU.subtract).then_inc(nm_split, 1)

            def normalise(t, k):
                dve.wait_ge(o_ready, t + 1)
                ov = ps_tt[:].rearrange("p u (j w) -> p (u j) w", j=UH)
                nc.vector.reciprocal(rden[k % 2][:], ov[:, :, DH]).then_inc(rden_ready, 1)
                dve.wait_ge(rden_ready, t + 1)
                tt(attn[k % 2][:], ov[:, :, 0:DH],
                   rden[k % 2][:].rearrange("p (h d) -> p h d", d=1).to_broadcast((P, H, DH)),
                   ALU.mult).then_inc(attn_ready, 1)

            def residual(t):
                dve.wait_ge(xb_ready, t + 1)
                dve.wait_ge(y_ready, t + 1)
                tt(X[:, t, :], X[:, t, :], ps_m[:, 256:384], ALU.add).then_inc(res_done, 1)

            dve.wait_ge(w_in, 16 * 16)
            dve.wait_ge(consts, 10)
            norm_x(0, 0)
            rotate(0, 0, 0)
            rotate(0, 0, 1)
            rotate(0, 1, 0)
            rotate(0, 1, 1)
            keep_v(0, 0)
            maxima(0, 0)
            split_maxima(0, 0)

            def step(n, k):
                g = group_after(n, k)
                par = (k // GB + 1) % 2
                b = k % GB
                more = not (known(n) and n == B - 1)
                tail = not (known(n) and n == 0)
                if more:
                    maxima(n + 1, (k + 1) % CYCLE)
                if tail:
                    normalise(n - 1, (k - 1) % CYCLE)
                if more:
                    split_maxima(n + 1, (k + 1) % CYCLE)
                if g is not None and b < 2:
                    rotate(g, b, 0)
                if g is not None and b < 2:
                    rotate(g, b, 1)
                if tail:
                    residual(n - 1)
                if g is not None and b == 0:
                    norm_x(g, par)
                if g is not None and b == 1:
                    keep_v(g, par)

            run_steps(dve, step)
            normalise(B - 1, CYCLE - 1)
            residual(B - 1)

            dve.wait_ge(ffn_in, 64)
            dve.wait_ge(res_done, B + 1)
            dve.sem_inc(relu_odd, 1)
            dve.sem_inc(acc_done, 2)
            with dve.Fori(0, NG) as g:
                layernorm(g + NG, xn[0], lambda t: X[:, g * GB + t, :], g + NG + 1, 10 * (g + NG))
                dve.wait_ge(xn_ready, GB * (g + NG + 1))
                chain = [ROUTE_OPS * g]

                def done(i, wait=True):
                    i.then_inc(route_op, 1)
                    chain[0] = chain[0] + 1

                def bc(ap, w):
                    return ap.to_broadcast((P, GB, w))

                tt(rt[:, :, 95:96], xn[0][:, :, 0:1], xn[0][:, :, 1:2], ALU.add).then_inc(route_op, 1)
                dve.wait_ge(route_op, ROUTE_OPS * g + 1)
                tt(rt[:, :, 0:17], bc(rt[:, :, 95:96], 17), steps_c[:, 0:17].rearrange("p (b j) -> p b j", b=1).to_broadcast((P, GB, 17)), ALU.is_ge).then_inc(route_op, 1)
                tt(rt[:, :, 17:34], bc(rt[:, :, 95:96], 17), steps_c[:, 17:34].rearrange("p (b j) -> p b j", b=1).to_broadcast((P, GB, 17)), ALU.is_gt).then_inc(route_op, 1)
                dve.wait_ge(route_op, ROUTE_OPS * g + 3)
                nc.vector.tensor_reduce(rt[:, :, 94], rt[:, :, 0:34], AX.X, ALU.add).then_inc(route_op, 1)
                dve.wait_ge(route_op, ROUTE_OPS * g + 4)
                tt(rt[:, :, 40:88], bc(rt[:, :, 94:95], 48), classes[:].rearrange("p (b j) -> p b j", b=1).to_broadcast((P, GB, 48)), ALU.is_equal).then_inc(route_op, 1)
                dve.wait_ge(route_op, ROUTE_OPS * g + 5)
                nc.vector.tensor_reduce(wt[:, :, 0, :], rt[:, :, 40:88].rearrange("p b (e k) -> p b e k", e=E_N), AX.X, ALU.add).then_inc(route_op, 1)
                dve.wait_ge(route_op, ROUTE_OPS * g + 6)
                tt(wt[:, :, 1, 1:E_N], wt[:, :, 0, 1:E_N], wt[:, :, 0, 0:E_N - 1], ALU.add).then_inc(route_op, 1)
                tt(wt[:, :, 1, 0:1], wt[:, :, 0, 0:1], wt[:, :, 0, E_N - 1:E_N], ALU.add).then_inc(route_op, 1)
                dve.wait_ge(route_op, ROUTE_OPS * g + 8)
                ts(wt[:, :, 2, :], wt[:, :, 1, :], 0.5, None, ALU.mult).then_inc(route_op, 1)
                dve.wait_ge(route_op, ROUTE_OPS * g + 9)
                dve.wait_ge(out_stored, 16 * (g + 1))
                for e in range(E_N):
                    if e:
                        dve.wait_ge(b2_done, GB * E_N * g + GB * e)
                    for t in range(GB):
                        nc.vector.scalar_tensor_tensor(acc[:, t, :], b2r[:, e, :], wt[:, t, 2, e:e + 1],
                                                       acc[:, t, :] if e else X[:, g * GB + t, :], ALU.mult,
                                                       ALU.add).then_inc(b2_done, 1)
                dve.wait_ge(b2_done, GB * E_N * (g + 1))

                def collect(e):
                    dve.wait_ge(acc_done, E_N * g + e + 2)
                    dve.wait_ge(ffn_y_ready, E_N * g + e + 3)
                    for t in range(GB):
                        i = nc.vector.scalar_tensor_tensor(acc[:, t, :], ps_t[:, e % 2, t * D:(t + 1) * D],
                                                           wt[:, t, 2, e:e + 1], acc[:, t, :], ALU.mult, ALU.add)
                    i.then_inc(acc_done, 1)

                for e in range(E_N):
                    for c in range(1, FC, 2):
                        if c == 1:
                            dve.wait_ge(ffn_y_ready, E_N * g + e + 1)
                        dve.wait_ge(h_odd, 16 * g + 2 * e + c // 2 + 1)
                        ts(hid[e % 2][:, c, :], ps_s[:, c % 2, :], b1c[:, e, c:c + 1], 0.0, ALU.add,
                           ALU.max).then_inc(relu_odd, 1)
                    if e:
                        collect(e - 1)
                collect(E_N - 1)


ROUTE_OPS = 9
_INS = ["x", "ctx_1024", "L0_xattn_bv", "L0_xattn_bo", "L0_ffn_W1", "L0_ffn_W2", "L0_ffn_b2"]


def kernel(**inputs):
    import concourse.bacc as bacc
    from concourse.bass_utils import run_bass_kernel_spmd

    nc = bacc.Bacc("TRN2", target_bir_lowering=False, num_devices=1)
    c = np.ascontiguousarray
    arrays = {n: c(inputs[n]) for n in _INS}
    swap = np.arange(D).reshape(D // 2, 2)[:, ::-1].reshape(D)
    for n in "kq":
        w = np.asarray(inputs[f"L0_xattn_W{n}"])
        arrays[f"W{n}T"] = c(w.T)
        arrays[f"W{n}sT"] = c(w[swap].T)
    for n in "vo":
        arrays[f"W{n}T"] = c(np.asarray(inputs[f"L0_xattn_W{n}"]).T)
    bk, bq = (np.asarray(inputs[f"L0_xattn_b{n}"]) for n in "kq")
    arrays["bcol"] = c(np.stack([bk, bk[swap], bq, bq[swap]], axis=1))
    arrays["b1c"] = c(np.asarray(inputs["L0_ffn_b1"]).reshape(E_N, FC, P).transpose(2, 0, 1))
    half = D // 2
    theta = np.float32(1250) ** (-np.arange(half, dtype=np.float32) / np.float32(half))
    ang = np.arange(L, dtype=np.float32)[:, None] * theta
    arrays["cosT"] = c(np.repeat(np.cos(ang), 2, axis=1).T.astype(np.float32))
    arrays["sinT"] = c(np.stack([-np.sin(ang), np.sin(ang)], axis=2).reshape(L, D).T.astype(np.float32))
    bf = mybir.dt.np(BF16)
    arrays["ident"] = np.eye(P, dtype=np.float32)
    arrays["bigI"] = (np.eye(P) * BIG).astype(bf)
    arrays["maskr"] = c(np.broadcast_to((np.triu(np.ones((L, L)), 1) * -BIG)[:, None, :], (P, UH, L)).astype(bf))
    j = np.arange(1, 18, dtype=np.float32)
    arrays["steps"] = np.concatenate([j, -j])[None, :]
    arrays["classes"] = (17 + np.arange(E_N)[:, None] + 8 * (np.arange(6)[None, :] - 3)).astype(np.float32).reshape(1, 48)
    aps = {n: nc.dram_tensor(f"in_{n}", v.shape, mybir.dt.from_np(v.dtype), kind="ExternalInput").ap()
           for n, v in arrays.items()}
    out = nc.dram_tensor("out_0", (B, L, D), F32, kind="ExternalOutput").ap()
    build(nc, aps, out)
    r = run_bass_kernel_spmd(nc, [{f"in_{n}": v for n, v in arrays.items()}], core_ids=[0])
    return r.results[0]["out_0"]
```

```python
from contextlib import ExitStack

import numpy as np

import concourse.bass as bass
from concourse import mybir

F32 = mybir.dt.float32
BF16 = mybir.dt.bfloat16
I32 = mybir.dt.int32
U32 = mybir.dt.uint32
ALU = mybir.AluOpType
ACT = mybir.ActivationFunctionType
AX = mybir.AxisListType

P = 128
B, L, D = 32, 128, 128
H, DH = 16, 8
HP = H // 2
GB = 4
NG = B // GB
GT = GB * L
UNITS = 4
UH = H // UNITS
PARTS = 3
Q_PART = (0, 1, 2, 0, 1, 0)
K_PART = (0, 0, 0, 1, 1, 2)
SLOTS = len(Q_PART)
HROWS = SLOTS * DH
PROWS = 2 * HROWS
MROWS = PROWS + 2
VW = 32
E_N, DFF = 8, 512
FC = DFF // P
EPS = 1e-5
SCALE = DH ** -0.5
BIG = 2.0 ** 15
CYCLE = 2 * GB
FIRST = GB + 1
LAST = GB
TOK = B * L
REGION = TOK + P
NT = (TOK + (E_N - 1) * (P - 1)) // P + 1
XW = 2 * D + 1
RING = 4
NTHR = 17


def build(nc, a, out):
    with ExitStack() as ctx:
        def sb(name, shape, dt=F32):
            return ctx.enter_context(nc.sbuf_tensor(name, shape, dt))

        def ps(name, shape):
            return ctx.enter_context(nc.psum_tensor(name, shape, F32))

        def sem(name):
            return ctx.enter_context(nc.semaphore(name))

        q_rows = nc.dram_tensor("q_rows", [H, PARTS, DH, GT], BF16, kind="Internal").ap()
        rows = nc.dram_tensor("rows", [E_N * REGION + P, XW], F32, kind="Internal").ap()
        k_rows = nc.dram_tensor("k_rows", [H, SLOTS, DH, GT], BF16, kind="Internal").ap()

        xin = [sb(f"xin{i}", [P, GB, D]) for i in range(2)]
        xb = [sb(f"xb{i}", [P, GB, D]) for i in range(2)]
        xr = [sb(f"xr{i}", [P, GB, XW]) for i in range(2)]
        ctxb = [sb(f"ctxb{i}", [P, GB, D]) for i in range(2)]
        xn = [sb(f"xn{i}", [P, GB, D]) for i in range(2)]
        xT = sb("xT", [P, GT])
        cT = sb("cT", [P, GT])
        rot1 = sb("rot1", [P, GB, L])
        rot2 = sb("rot2", [P, GB, L])
        rot = [sb(f"rot{i}", [P, GT]) for i in "kq"]
        rest = sb("rest", [P, GT])
        parts = [sb(f"parts_{i}", [P, PARTS, GT], BF16) for i in "kq"]
        qst = [sb(f"qst{i}", [P, HP, 2, GT], BF16) for i in range(2)]
        kst = [sb(f"kst{i}", [P, HP, GT], BF16) for i in range(2)]
        vaug = [sb(f"vaug{i}", [P, GB, H, VW]) for i in range(2)]
        ex = [sb(f"ex{i}", [P, H, L]) for i in range(2)]
        oT = sb("oT", [P, UNITS, L])
        attn = [sb(f"attn{i}", [P, H, DH]) for i in range(2)]
        attnT = sb("attnT", [P, L])
        nmax = [sb(f"nmax{i}", [P, H]) for i in range(2)]
        nmh = [sb(f"nmh{i}", [H, 2, L], BF16) for i in range(2)]
        rden = [sb(f"rden{i}", [P, H]) for i in range(2)]
        stats = sb("stats", [P, GB, 6])
        lnb = sb("lnb", [P, 8, GB])
        stats2 = sb("stats2", [P, GB, 6])
        ln2b = sb("ln2b", [P, 8, GB])
        gate = sb("gate", [P, 2 * CYCLE + 2 + RING])
        ident = sb("ident", [P, P])
        bigI = sb("bigI", [P, P], BF16)
        maskr = sb("maskr", [P, UH, L], BF16)
        wk = sb("wk", [P, D])
        wks = sb("wks", [P, D])
        wq = sb("wq", [P, D])
        wqs = sb("wqs", [P, D])
        wv = sb("wv", [P, D])
        wo = sb("wo", [P, D])
        cosT = sb("cosT", [P, L])
        sinT = sb("sinT", [P, L])
        bcol = sb("bcol", [P, 4])
        bvr = sb("bvr", [P, D])
        bor = sb("bor", [P, D])
        w1 = sb("w1", [P, E_N + 1, DFF + FC])
        w2 = sb("w2", [P, E_N + 1, FC, D])
        b2r = sb("b2r", [P, E_N + 1, D])
        b2h = sb("b2h", [P, E_N, D])
        thr = sb("thr", [P, 2 * NTHR])
        classes = sb("classes", [P, 48])
        rt = sb("rt", [P, GB, 96])
        oh = [sb(f"oh{i}", [P, GB, E_N], BF16) for i in range(2)]
        ohf = sb("ohf", [P, GB, E_N])
        tri = sb("tri", [P, P], BF16)
        ones = sb("ones", [P, P], BF16)
        place = [sb(f"place{i}", [P, E_N]) for i in range(2)]
        place0 = sb("place_first", [P, E_N])
        at = sb("at", [P, GB, E_N])
        at2 = sb("at2", [P, GB, E_N])
        rowf = sb("rowf", [P, GB])
        rowi = [sb(f"rowi{i}", [P, GB], I32) for i in range(2)]
        tok = [sb(f"tok{i}", [P, GB]) for i in range(2)]
        lane = sb("lane", [P, 1])
        pad = sb("pad", [P, XW])
        padf = sb("padf", [P, E_N])
        padi = sb("padi", [P, E_N], I32)
        k128 = sb("k128", [P, 32])
        lower = sb("lower", [P, E_N, E_N])
        tile_no = sb("tile_no", [P, NT])
        cnt = sb("cnt", [P, E_N])
        big_a = sb("big_a", [P, NT * E_N])
        big_b = sb("big_b", [P, NT * E_N])
        tiles_of = sb("tiles_of", [P, E_N])
        upto = sb("upto", [P, E_N])
        tcls = sb("tcls", [P, NT])
        tbef = sb("tbef", [P, NT])
        trow = sb("trow", [P, NT])
        tcls_i = sb("tcls_i", [P, NT], I32)
        trow_i = sb("trow_i", [P, NT], I32)
        xt = [qst[0][:, i, :, :].rearrange("p a t -> p (a t)").bitcast(F32)[:, 0:XW] for i in range(RING)]
        w1s = [ex[i][:].rearrange("p h l -> p (h l)")[:, 0:2 * (DFF + FC)].rearrange("p (e f) -> p e f", e=2) for i in range(2)]
        hid = [[kst[i][:, 2 * e:2 * e + 2, :].rearrange("p a t -> p (a t)").bitcast(F32).rearrange("p (c t) -> p c t", c=FC)
                for e in range(2)] for i in range(2)]
        xtT = [xn[i][:, 0, :] for i in range(2)]

        ps_s = ps("ps_s", [P, 2, UH * L])
        ps_t = ps("ps_t", [P, 2, UH * L])
        ps_o = ps("ps_o", [P, UNITS, L])
        ps_tt = ps("ps_tt", [P, UNITS, P])
        ps_a = ps("ps_a", [P, GT])
        ps_m = ps("ps_m", [P, 512])

        x_in = [sem(f"x_in{i}") for i in range(2)]
        ffn_in = sem("ffn_in")
        route_in = sem("route_in")
        place_read = sem("place_read")
        xb_ready = sem("xb_ready")
        w_in = sem("w_in")
        ctx_in = [sem(f"ctx_in{i}") for i in range(2)]
        consts = sem("consts")
        var_ready = sem("var_ready")
        rstd_ready = sem("rstd_ready")
        ln_op = sem("ln_op")
        xn_ready = sem("xn_ready")
        ctxT_ready = sem("ctxT_ready")
        ctxT_in_sb = sem("ctxT_in_sb")
        xT_ready = sem("xT_ready")
        xT_in_sb = sem("xT_in_sb")
        proj_ready = sem("proj_ready")
        cos_done = sem("cos_done")
        sin_done = sem("sin_done")
        rot_ready = sem("rot_ready")
        part0_ready = sem("part0_ready")
        rest_ready = sem("rest_ready")
        part1_ready = sem("part1_ready")
        part2_ready = sem("part2_ready")
        vproj_ready = sem("vproj_ready")
        v_ready = sem("v_ready")
        k_out = sem("k_out")
        q_out = sem("q_out")
        stacks_in = sem("stacks_in")
        s_ready = sem("s_ready")
        max_done = sem("max_done")
        nmT_ready = sem("nmT_ready")
        nm0_ready = sem("nm0_ready")
        nm_split = sem("nm_split")
        nm_rows = sem("nm_rows")
        st_ready = sem("st_ready")
        exp_done = sem("exp_done")
        mask_done = sem("mask_done")
        pv_done = sem("pv_done")
        oT_in_sb = sem("oT_in_sb")
        o_ready = sem("o_ready")
        rden_ready = sem("rden_ready")
        attn_ready = sem("attn_ready")
        attnT_ready = sem("attnT_ready")
        attnT_in_sb = sem("attnT_in_sb")
        y_ready = sem("y_ready")
        res_done = sem("res_done")
        ln2_op = sem("ln2_op")
        var2_ready = sem("var2_ready")
        rstd2_ready = sem("rstd2_ready")
        xn2_ready = sem("xn2_ready")
        route_op = sem("route_op")
        oh_ready = sem("oh_ready")
        rank_ready = sem("rank_ready")
        place_op = sem("place_op")
        rowi_ready = sem("rowi_ready")
        rows_out = sem("rows_out")
        pads_out = sem("pads_out")
        spare_out = sem("spare_out")
        table_op = sem("table_op")
        pad_ready = sem("pad_ready")
        table_ready = sem("table_ready")
        tile_in = [sem(f"tile_in{i}") for i in range(RING)]
        w1_staged = sem("w1_staged")
        b2_added = sem("b2_added")
        xt_T_ready = sem("xt_T_ready")
        xt_T_in_sb = sem("xt_T_in_sb")
        h0_ready = sem("h0_ready")
        h1_ready = sem("h1_ready")
        relu0 = sem("relu0")
        relu1 = sem("relu1")
        y2_ready = sem("y2_ready")
        fin_done = sem("fin_done")
        gate_passed = sem("gate_passed")
        out_stored = [sem(f"out_stored{i}") for i in range(RING)]

        block = ctx.enter_context(nc.Block())

        def run_steps(eng, step):
            def alone(n):
                g = n // GB
                step(n, n % CYCLE, g - 1 if g else None, g + 1 if g + 1 < NG else None)

            for n in range(FIRST):
                alone(n)
            whole = (B - FIRST - LAST) // CYCLE
            with eng.Fori(0, whole) as c:
                for k in range(FIRST, FIRST + CYCLE):
                    step(c * CYCLE + k, k % CYCLE, c * 2 + (k // GB - 1), c * 2 + (k // GB + 1))
            for n in range(FIRST + whole * CYCLE, B):
                alone(n)

        def run_tiles(eng, tile):
            with eng.Fori(0, (NT - RING) // RING) as q:
                for k in range(1, RING + 1):
                    tile(q * RING + k, k % RING)
            for j in range((NT - RING) // RING * RING + 1, NT):
                tile(j, j % RING)

        def laps(j, r):
            return 16 * (j // RING) if known(j) else (16 // RING) * (j - r)

        def known(n):
            return isinstance(n, int)

        @block.sync
        def _(sp):
            xv = a["x"].rearrange("b l d -> l b d")
            cv = a["ctx_1024"].rearrange("b l d -> l b d")

            def load_ctx(g, par):
                sp.dma_start(ctxb[par][:], cv[:, bass.ts(g, GB), :]).then_inc(ctx_in[par], 16)

            def load_x(g, par):
                sp.dma_start(xin[par][:], xv[:, bass.ts(g, GB), :]).then_inc(x_in[par], 16)

            sp.dma_start(ident[:], a["ident"]).then_inc(w_in, 16)
            load_ctx(0, 0)
            load_x(0, 0)
            for t, n in ((wk, "WkT"), (wks, "WksT"), (wq, "WqT"), (wqs, "WqsT"), (wv, "WvT"), (wo, "WoT"),
                         (cosT, "cosT"), (sinT, "sinT"), (bcol, "bcol"), (bigI, "bigI"), (maskr, "maskr")):
                sp.dma_start(t[:], a[n]).then_inc(w_in, 16)
            sp.dma_start(bvr[:], a["L0_xattn_bv"].rearrange("(a d) -> a d", a=1).to_broadcast((P, D))).then_inc(w_in, 16)
            sp.dma_start(bor[:], a["L0_xattn_bo"].rearrange("(a d) -> a d", a=1).to_broadcast((P, D))).then_inc(w_in, 16)
            load_ctx(1, 1)
            load_x(1, 1)
            for t, n, w in ((thr, "thr", 2 * NTHR), (classes, "classes", 48), (place0, "place0", E_N), (place[1], "place0", E_N), (k128, "k128", 32),
                            (tile_no, "tile_no", NT)):
                sp.dma_start(t[:], a[n].to_broadcast((P, w))).then_inc(route_in, 16)
            sp.dma_start(lower[:], a["lower"].to_broadcast((P, E_N, E_N))).then_inc(route_in, 16)
            for t, n in ((tri, "tri"), (ones, "ones"), (lane, "lane"), (pad, "pad"), (tok[1], "tok")):
                sp.dma_start(t[:], a[n]).then_inc(route_in, 16)
            for e0, e1 in ((0, E_N), (E_N, E_N + 1)):
                n = e1 - e0
                sp.dma_start(w1[:, e0:e1, 0:DFF], a["L0_ffn_W1"][0:n].rearrange("e d f -> d e f")).then_inc(ffn_in, 16)
                sp.dma_start(w1[:, e0:e1, DFF:DFF + FC], a["b1c"][:, 0:n, :]).then_inc(ffn_in, 16)
                sp.dma_start(w2[:, e0:e1], a["L0_ffn_W2"][0:n].rearrange("e (c p) d -> p e c d", p=P)).then_inc(ffn_in, 16)
                sp.dma_start(b2r[:, e0:e1, :], a["L0_ffn_b2"][0:n].rearrange("(a e) d -> a e d", a=1).to_broadcast((P, n, D))).then_inc(ffn_in, 16)
            sp.wait_ge(route_in, 16 * ROUTE_IN)
            sp.dma_start(rows[E_N * REGION:E_N * REGION + P, :], pad[:]).then_inc(spare_out, 16)

            def k_stack(g, par):
                if not (known(g) and g == 0):
                    sp.wait_ge(stacks_in, 16 * 8 * g)
                sp.wait_ge(part2_ready, 2 * g + 1)
                for s in range(SLOTS):
                    sp.dma_start(k_rows[:, s], parts[0][:, K_PART[s], :]).then_inc(k_out, 16)
                sp.wait_ge(k_out, 16 * SLOTS * (g + 1))
                for m in range(2):
                    sp.dma_start(kst[par][m * HROWS:(m + 1) * HROWS, :, :],
                                 k_rows.rearrange("(g m) s r t -> m (s r) g t", m=2)[m]).then_inc(stacks_in, 16)

            def q_stack(g, par):
                sp.wait_ge(part2_ready, 2 * g + 2)
                for s in range(PARTS):
                    sp.dma_start(q_rows[:, s], parts[1][:, s, :]).then_inc(q_out, 16)
                sp.wait_ge(q_out, 16 * PARTS * (g + 1))
                for m in range(2):
                    qv = q_rows.rearrange("(g m) s r t -> m (s r) g t", m=2)[m]
                    at = m * HROWS
                    for w in (PARTS, 2, 1):
                        sp.dma_start(qst[par][at:at + w * DH, :, m, :], qv[0:w * DH]).then_inc(stacks_in, 16)
                        at += w * DH

            def maxima_rows(m, k):
                sp.wait_ge(nm_split, m + 1)
                b = k % GB
                for s in range(2):
                    sp.dma_start(qst[k // GB][PROWS + s:PROWS + s + 1, :, :, b * L:(b + 1) * L],
                                 nmh[k % 2][:, s, :]).then_inc(nm_rows, 16)

            sp.wait_ge(consts, 6)
            k_stack(0, 0)
            q_stack(0, 0)
            maxima_rows(0, 0)

            def step(n, k, r, g):
                par = (k // GB + 1) % 2
                b = k % GB
                if g is not None and b == 1:
                    k_stack(g, par)
                if not (known(n) and n == B - 1):
                    maxima_rows(n + 1, (k + 1) % CYCLE)
                if g is not None and b == 2:
                    q_stack(g, par)
                    if not (known(g) and g + 1 >= NG):
                        sp.wait_ge(ctxT_ready, g)
                        load_ctx(g + 1, 1 - par)
                        sp.wait_ge(xb_ready, g)
                        load_x(g + 1, 1 - par)

            run_steps(sp, step)

            def load_tile(j, r):
                row = sp.value_load(trow_i[0:1, bass.ds(j, 1)], min_val=0, max_val=E_N * REGION)
                sp.dma_start(xt[r], rows[bass.ds(row, P), :]).then_inc(tile_in[r], 16)

            sp.wait_ge(table_ready, 1)
            sp.wait_ge(rows_out, 16 * B)
            sp.wait_ge(spare_out, 16)
            sp.wait_ge(pads_out, 16 * E_N)
            for j in range(RING):
                load_tile(j, j)

            def tile(j, r):
                if known(j) and j + RING - 1 >= NT:
                    return
                sp.wait_ge(out_stored[(r - 1) % RING], laps(j - 1, (r - 1) % RING) + 16)
                load_tile(j + RING - 1, (r - 1) % RING)

            run_tiles(sp, tile)
            for r in range(RING):
                sp.wait_ge(out_stored[r], 16 * ((NT - 1 - r) // RING + 1))

        @block.gpsimd
        def _(pool):
            for i in range(2):
                nc.gpsimd.memset(qst[i][:], 0.0).then_inc(consts, 1)
            for i in range(2):
                nc.gpsimd.memset(kst[i][:], 1.0).then_inc(consts, 1)
            for i in range(2):
                nc.gpsimd.memset(vaug[i][:], 0.0).then_inc(consts, 1)
            pool.wait_ge(consts, 6)
            for i in range(2):
                nc.gpsimd.memset(vaug[i][:, :, :, DH:DH + 1], 1.0).then_inc(consts, 1)
            nc.gpsimd.memset(lnb[:, 7, :], -0.5).then_inc(consts, 1)
            nc.gpsimd.memset(gate[:], 0.0).then_inc(consts, 1)
            pool.wait_ge(consts, 10)

            def pass_gate(j):
                return nc.gpsimd.tensor_tensor(gate[:, j:j + 1], lnb[:, 7, 0:1], lnb[:, 7, 0:1], ALU.add)

            def rstd2(g):
                pool.wait_ge(var2_ready, g + 1)
                nc.gpsimd.tensor_tensor(ln2b[:, 6, :], ln2b[:, 5, :], lnb[:, 7, :], ALU.pow).then_inc(rstd2_ready, 1)

            def scatter(g, par):
                pool.wait_ge(rowi_ready, g + 1)
                pass_gate(2 * CYCLE + par)
                for t in range(GB):
                    nc.gpsimd.indirect_dma_start(rows, bass.IndirectOffsetOnAxis(ap=rowi[par][:, t:t + 1], axis=0),
                                                 xr[par][:, t, :], None).then_inc(rows_out, 16)

            def rstd(g):
                pool.wait_ge(var_ready, g + 1)
                nc.gpsimd.tensor_tensor(lnb[:, 6, :], lnb[:, 5, :], lnb[:, 7, :], ALU.pow).then_inc(rstd_ready, 1)

            def split(g, i):
                pool.wait_ge(sin_done, 2 * g + i + 1)
                nc.gpsimd.tensor_tensor(rot[i][:], rot1[:].rearrange("p b l -> p (b l)"),
                                        rot2[:].rearrange("p b l -> p (b l)"), ALU.add).then_inc(rot_ready, 1)
                pool.wait_ge(part0_ready, 2 * g + i + 1)
                nc.gpsimd.tensor_tensor(rest[:], rot[i][:], parts[i][:, 0, :], ALU.subtract).then_inc(rest_ready, 1)
                pool.wait_ge(part1_ready, 2 * g + i + 1)
                nc.gpsimd.tensor_tensor(parts[i][:, 2, :], rest[:], parts[i][:, 1, :],
                                        ALU.subtract).then_inc(part2_ready, 1)

            def mask(n, k, u):
                pool.wait_ge(exp_done, UNITS * n + u + 1)
                pass_gate((k * UNITS + u) % (2 * CYCLE))
                e = ex[k % 2][:, u * UH:(u + 1) * UH, :]
                nc.gpsimd.affine_select(out=e, in_=e, pattern=[[0, UH], [1, L]], compare_op=ALU.is_ge, fill=0.0,
                                        base=0, channel_multiplier=-1).then_inc(mask_done, 1)

            rstd(0)
            split(0, 0)
            split(0, 1)

            def step(n, k, r, g):
                b = k % GB
                for u in range(UNITS):
                    mask(n, k, u)
                    if g is not None and b == 0 and u == 3:
                        split(g, 0)
                        rstd(g)
                    if g is not None and b == 1 and u == 3:
                        split(g, 1)
                    if r is not None and b == 2 and u == 3:
                        rstd2(r)
                if r is not None and b == 3:
                    scatter(r, (k // GB + 1) % 2)

            run_steps(pool, step)
            rstd2(NG - 1)
            scatter(NG - 1, (NG - 1) % 2)
            pool.wait_ge(pad_ready, 1)
            for e in range(E_N):
                nc.gpsimd.indirect_dma_start(rows, bass.IndirectOffsetOnAxis(ap=padi[:, e:e + 1], axis=0),
                                             pad[:], None).then_inc(pads_out, 16)

            def store(j, r):
                pool.wait_ge(gate_passed, j + 1)
                pool.wait_ge(fin_done, j + 3)
                pass_gate(2 * CYCLE + 2 + r).then_inc(gate_passed, 1)
                nc.gpsimd.indirect_dma_start(out.rearrange("b l d -> (b l) d"),
                                             bass.IndirectOffsetOnAxis(ap=xt[r][:, 2 * D:XW].bitcast(U32), axis=0),
                                             xt[r][:, 0:D], None, bounds_check=TOK - 1,
                                             oob_is_err=False).then_inc(out_stored[r], 16)

            pool.sem_inc(gate_passed, RING)
            run_tiles(pool, lambda j, r: store(j - 1, (r - 1) % RING))
            store(NT - 1, (NT - 1) % RING)

        @block.scalar
        def _(act):
            def evac_ctxT(g):
                act.wait_ge(ctxT_ready, g + 1)
                nc.scalar.activation(cT[:], ps_a[:], ACT.Copy).then_inc(ctxT_in_sb, 1)

            def evac_xT(g):
                act.wait_ge(xT_ready, g + 1)
                nc.scalar.activation(xT[:], ps_a[:], ACT.Copy).then_inc(xT_in_sb, 1)

            def split(g, i):
                if not (known(g) and g == 0):
                    act.wait_ge((k_out, q_out)[i], 16 * (SLOTS, PARTS)[i] * g)
                act.wait_ge(rot_ready, 2 * g + i + 1)
                nc.scalar.activation(parts[i][:, 0, :], rot[i][:], ACT.Copy).then_inc(part0_ready, 1)
                act.wait_ge(rest_ready, 2 * g + i + 1)
                nc.scalar.activation(parts[i][:, 1, :], rest[:], ACT.Copy).then_inc(part1_ready, 1)

            def exp(n, k, u):
                if u == 0 and not (known(n) and n == 0):
                    act.wait_ge(pv_done, n)
                act.wait_ge(st_ready, UNITS * n + u + 1)
                nc.scalar.activation(ex[k % 2][:, u * UH:(u + 1) * UH, :],
                                     ps_t[:, u % 2, :].rearrange("p (h l) -> p h l", h=UH),
                                     ACT.Exp, scale=SCALE).then_inc(exp_done, 1)

            def evac_o(n):
                act.wait_ge(pv_done, n + 2)
                nc.scalar.activation(oT[:], ps_o[:], ACT.Copy).then_inc(oT_in_sb, 1)

            def evac_attnT(t):
                act.wait_ge(attnT_ready, t + 1)
                nc.scalar.activation(attnT[:], ps_m[:, 128:256], ACT.Copy).then_inc(attnT_in_sb, 1)

            evac_ctxT(0)
            evac_xT(0)
            split(0, 0)
            split(0, 1)

            def step(n, k, r, g):
                b = k % GB
                if g is not None and b == 0:
                    evac_ctxT(g)
                if g is not None and b == 1:
                    evac_xT(g)
                exp(n, k, 0)
                exp(n, k, 1)
                if not (known(n) and n == 0):
                    evac_attnT(n - 1)
                exp(n, k, 2)
                exp(n, k, 3)
                evac_o(n)
                if g is not None and b < 2:
                    split(g, b)

            run_steps(act, step)
            evac_attnT(B - 1)

            def evac_tile(j, r):
                act.wait_ge(xt_T_ready, j + 1)
                nc.scalar.activation(xtT[r % 2], (ps_a[:, 0:P], ps_m[:, 0:P])[r % 2], ACT.Copy).then_inc(xt_T_in_sb, 1)

            def relu(j, r):
                act.wait_ge(h0_ready, j + 1)
                if not (known(j) and j == 0):
                    act.wait_ge(y2_ready, j)
                for c in range(FC):
                    i = nc.scalar.activation(hid[r % 2][0][:, c, :], (ps_s, ps_t)[r % 2][:, 0, c * P:(c + 1) * P],
                                             ACT.Relu, bias=w1s[r % 2][:, 0, DFF + c:DFF + c + 1])
                i.then_inc(relu0, 1)

            evac_tile(0, 0)
            evac_tile(1, 1)
            relu(0, 0)

            def tile(j, r):
                if not (known(j) and j + 1 >= NT):
                    evac_tile(j + 1, (r + 1) % RING)
                relu(j, r)

            run_tiles(act, tile)

        @block.tensor
        def _(pe):
            mm, tr = nc.tensor.matmul, nc.tensor.transpose
            pe.sem_inc(pv_done, 1)

            def ctx_transpose(g, par):
                pe.wait_ge(ctx_in[par], 8 * (g - par) + 16)
                if known(g) and 0 < g < 3:
                    pe.wait_ge(v_ready, g)
                elif not (known(g) and g == 0):
                    pe.wait_ge(place_read, g - 2)
                for t in range(GB):
                    i = tr(ps_a[:, t * L:(t + 1) * L], ctxb[par][:, t, :], ident[:])
                i.then_inc(ctxT_ready, 1)

            def x_transpose(g, par):
                pe.wait_ge(xn_ready, GB * (g + 1))
                pe.wait_ge(sin_done, 2 * g + 1)
                for t in range(GB):
                    i = tr(ps_a[:, t * L:(t + 1) * L], xn[par][:, t, :], ident[:])
                i.then_inc(xT_ready, 1)

            def project(g, i):
                pe.wait_ge((ctxT_in_sb, cos_done, xT_in_sb, cos_done)[i], (g + 1, 2 * g + 1, g + 1, 2 * g + 2)[i])
                mm(ps_a[:], (wk, wks, wq, wqs)[i][:], (cT, cT, xT, xT)[i][:], start=True, stop=True).then_inc(proj_ready, 1)

            def project_v(g):
                pe.wait_ge(sin_done, 2 * g + 2)
                for t in range(GB):
                    i = mm(ps_a[:, t * L:(t + 1) * L], cT[:, t * L:(t + 1) * L], wv[:], start=True, stop=True)
                i.then_inc(vproj_ready, 1)

            def scores(m, k):
                b, par = k % GB, k // GB
                tok = slice(b * L, (b + 1) * L)
                for u in range(UNITS):
                    if u == 0 and b == 0:
                        pe.wait_ge(stacks_in, 16 * 8 * (m // GB + 1) if known(m) else 32 * (m + GB))
                    if not (known(m) and m * UNITS + u < 2):
                        pe.wait_ge(max_done, UNITS * m + u - 1)
                    bank = ps_s[:, u % 2, :]
                    mm(bank, bigI[:], maskr[:].rearrange("p h l -> p (h l)"), start=True, stop=False, skip_group_check=True)
                    for j in range(UH):
                        h = u * UH + j
                        i = mm(bank[:, j * L:(j + 1) * L], qst[par][0:PROWS, h // 2, h % 2, tok],
                               kst[par][0:PROWS, h // 2, tok], start=False, stop=(j == UH - 1), skip_group_check=True)
                    i.then_inc(s_ready, 1)

            def maxima_transpose(m, k):
                pe.wait_ge(max_done, UNITS * (m + 1))
                if not (known(m) and m == 0):
                    pe.wait_ge(nm_split, m)
                if not (known(m) and m < 2):
                    pe.wait_ge(res_done, m - 1)
                tr(ps_m[0:H, 0:L], nmax[k % 2][:], ident[:]).then_inc(nmT_ready, 1)

            def scores_t(n, k, u):
                b, par = k % GB, k // GB
                tok = slice(b * L, (b + 1) * L)
                if u == 0:
                    pe.wait_ge(nm_rows, 32 * (n + 1))
                if not (known(n) and n * UNITS + u < 2):
                    pe.wait_ge(exp_done, UNITS * n + u - 1)
                for j in range(2):
                    g = 2 * u + j
                    i = mm(ps_t[:, u % 2, j * 2 * L:(j + 1) * 2 * L], kst[par][0:MROWS, g, tok],
                           qst[par][0:MROWS, g, :, tok], start=True, stop=True)
                i.then_inc(st_ready, 1)

            def weigh_v(n, k, u):
                b, par = k % GB, k // GB
                if u == 0:
                    pe.wait_ge(v_ready, n // GB + 1 if known(n) else (n - b) // GB + 1)
                    if not (known(n) and n == 0):
                        pe.wait_ge(oT_in_sb, n)
                pe.wait_ge(mask_done, UNITS * n + u + 1)
                for j in range(UH):
                    h = u * UH + j
                    i = mm(ps_o[j * VW:(j + 1) * VW, u, :], vaug[par][:, b, h, :], ex[k % 2][:, h, :], start=True, stop=True)
                if u == UNITS - 1:
                    i.then_inc(pv_done, 1)

            def o_transpose(t):
                pe.wait_ge(oT_in_sb, t + 1)
                if not (known(t) and t == 0):
                    pe.wait_ge(attn_ready, t + 1)
                for u in range(UNITS):
                    i = tr(ps_tt[:, u, :], oT[:, u, :], ident[:])
                i.then_inc(o_ready, 1)

            def attn_transpose(t, k):
                pe.wait_ge(attn_ready, t + 2)
                if known(t) and t + 2 >= B:
                    pe.wait_ge(res_done, t + 1)
                else:
                    pe.wait_ge(nm_split, t + 3)
                tr(ps_m[:, 128:256], attn[k % 2][:].rearrange("p h d -> p (h d)"), ident[:]).then_inc(attnT_ready, 1)

            def project_o(t):
                pe.wait_ge(attnT_in_sb, t + 2)
                mm(ps_m[:, 256:384], attnT[:], wo[:], start=True, stop=True).then_inc(y_ready, 1)

            def ranks(g, par):
                pe.wait_ge(oh_ready, g + 1)
                pe.wait_ge(v_ready, min(g + 3, NG) if known(g) else g + 3)
                o = ps_a[:, 0:(GB + 1) * E_N].rearrange("p (t e) -> p t e", e=E_N)
                mm(o[:, 0:GB, :], tri[:], oh[par][:], start=True, stop=False, skip_group_check=True)
                for t in range(GB):
                    i = mm(o[:, t + 1:GB + 1, :], ones[:], oh[par][:, t:t + 1, :].to_broadcast((P, GB - t, E_N)),
                           start=False, stop=(t == GB - 1), skip_group_check=True)
                i.then_inc(rank_ready, 1)

            pe.wait_ge(w_in, 16 * W_IN)
            ctx_transpose(0, 0)
            project(0, 0)
            project(0, 1)
            x_transpose(0, 0)
            project(0, 2)
            project(0, 3)
            project_v(0)
            pe.wait_ge(consts, 10)
            scores(0, 0)
            maxima_transpose(0, 0)

            def step(n, k, r, g):
                par = (k // GB + 1) % 2
                b = k % GB
                more = not (known(n) and n == B - 1)
                tail = not (known(n) and n == 0)
                stage_a = [] if g is None else {
                    0: [lambda: ctx_transpose(g, par), lambda: project(g, 0), lambda: project(g, 1), None],
                    1: [lambda: x_transpose(g, par), lambda: project(g, 2), lambda: project(g, 3),
                        lambda: project_v(g)]}.get(b, [])

                def a_piece(i):
                    if i < len(stage_a) and stage_a[i]:
                        stage_a[i]()

                if more:
                    scores(n + 1, (k + 1) % CYCLE)
                a_piece(0)
                if tail:
                    o_transpose(n - 1)
                scores_t(n, k, 0)
                scores_t(n, k, 1)
                if more:
                    maxima_transpose(n + 1, (k + 1) % CYCLE)
                weigh_v(n, k, 0)
                a_piece(1)
                if tail:
                    attn_transpose(n - 1, (k - 1) % CYCLE)
                scores_t(n, k, 2)
                weigh_v(n, k, 1)
                a_piece(2)
                scores_t(n, k, 3)
                if tail:
                    project_o(n - 1)
                weigh_v(n, k, 2)
                a_piece(3)
                weigh_v(n, k, 3)
                if r is not None and b == 3:
                    ranks(r, (k // GB + 1) % 2)

            run_steps(pe, step)
            o_transpose(B - 1)
            attn_transpose(B - 1, CYCLE - 1)
            project_o(B - 1)
            ranks(NG - 1, (NG - 1) % 2)

            def tile_transpose(j, r):
                pe.wait_ge(tile_in[r], laps(j, r) + 16)
                tr((ps_a[:, 0:P], ps_m[:, 0:P])[r % 2], xt[r][:, D:2 * D], ident[:]).then_inc(xt_T_ready, 1)

            def up(j, r):
                pe.wait_ge(w1_staged, j + 1)
                pe.wait_ge(xt_T_in_sb, j + 1)
                for e in range(2):
                    for c in range(FC):
                        i = mm((ps_s, ps_t)[r % 2][:, e, c * P:(c + 1) * P], w1s[r % 2][:, e, c * P:(c + 1) * P],
                               xtT[r % 2], start=True, stop=True)
                    i.then_inc((h0_ready, h1_ready)[e], 1)

            def down(j, r):
                cls = pe.value_load(tcls_i[0:1, bass.ds(j, 1)], min_val=0, max_val=E_N - 1)
                y = (ps_o, ps_tt)[r % 2][:, 0, :]
                pe.wait_ge(fin_done, j + 1)
                for e in range(2):
                    pe.wait_ge((relu0, relu1)[e], j + 1)
                    for c in range(FC):
                        i = mm(y, hid[r % 2][e][:, c, :], w2[:, bass.ds(cls + e, 1), c, :].rearrange("p e d -> p (e d)"),
                               start=(e == 0 and c == 0), stop=(e == 1 and c == FC - 1))
                i.then_inc(y2_ready, 1)

            pe.sem_inc(y2_ready, 1)
            pe.wait_ge(place_read, NG)
            pe.wait_ge(res_done, B + 1)
            pe.wait_ge(table_ready, 1)
            tile_transpose(0, 0)
            tile_transpose(1, 1)
            up(0, 0)

            def tile(j, r):
                if not (known(j) and j + 1 >= NT):
                    tile_transpose(j + 1, (r + 1) % RING)
                up(j, r)
                down(j - 1, (r - 1) % RING)

            run_tiles(pe, tile)
            down(NT - 1, (NT - 1) % RING)

        @block.vector
        def _(dve):
            tt, ts = nc.vector.tensor_tensor, nc.vector.tensor_scalar
            dve.sem_inc(attn_ready, 1)
            dve.sem_inc(res_done, 1)
            dve.sem_inc(attnT_in_sb, 1)

            def variances(g, b, st, x_at, op, var_done):
                base = 10 * g
                for t in range(GB):
                    nc.vector.bn_stats(st[:, t, :], x_at(t)).then_inc(op, 1)
                dve.wait_ge(op, base + 4)
                tt(b[:, 0, :], st[:, :, 1], st[:, :, 4], ALU.add).then_inc(op, 1)
                tt(b[:, 1, :], st[:, :, 1], st[:, :, 4], ALU.subtract).then_inc(op, 1)
                tt(b[:, 2, :], st[:, :, 2], st[:, :, 5], ALU.add).then_inc(op, 1)
                dve.wait_ge(op, base + 7)
                ts(b[:, 0, :], b[:, 0, :], 0.5, None, ALU.mult).then_inc(op, 1)
                tt(b[:, 3, :], b[:, 1, :], b[:, 1, :], ALU.mult).then_inc(op, 1)
                ts(b[:, 4, :], b[:, 2, :], 1.0 / D, EPS, ALU.mult, ALU.add).then_inc(op, 1)
                dve.wait_ge(op, base + 10)
                nc.vector.scalar_tensor_tensor(b[:, 5, :], b[:, 3, :], 0.25, b[:, 4, :], ALU.mult,
                                               ALU.add).then_inc(var_done, 1)

            def norm_x(g, par):
                dve.wait_ge(x_in[par], 8 * (g - par) + 16)
                variances(g, lnb, stats, lambda t: xin[par][:, t, :], ln_op, var_ready)
                dve.wait_ge(rstd_ready, g + 1)
                for t in range(GB):
                    ts(xn[par][:, t, :], xin[par][:, t, :], lnb[:, 0, t:t + 1], lnb[:, 6, t:t + 1], ALU.subtract,
                       ALU.mult).then_inc(xn_ready, 1)
                tt(xb[par][:], xin[par][:], bor[:].rearrange("p (b d) -> p b d", b=1).to_broadcast((P, GB, D)),
                   ALU.add).then_inc(xb_ready, 1)

            def route_stats(g, par):
                dve.wait_ge(res_done, GB * (g + 1) + 1)
                variances(g, ln2b, stats2, lambda t: xr[par][:, t, 0:D], ln2_op, var2_ready)

            def route_class(g, par):
                dve.wait_ge(rstd2_ready, g + 1)
                for t in range(GB):
                    ts(xr[par][:, t, D:2 * D], xr[par][:, t, 0:D], ln2b[:, 0, t:t + 1], ln2b[:, 6, t:t + 1],
                       ALU.subtract, ALU.mult).then_inc(xn2_ready, 1)
                base = 6 * g
                dve.wait_ge(xn2_ready, GB * (g + 1))
                tt(rt[:, :, 95:96], xr[par][:, :, D:D + 1], xr[par][:, :, D + 1:D + 2], ALU.add).then_inc(route_op, 1)
                dve.wait_ge(route_op, base + 1)
                for i, op in enumerate((ALU.is_ge, ALU.is_gt)):
                    tt(rt[:, :, i * NTHR:(i + 1) * NTHR], rt[:, :, 95:96].to_broadcast((P, GB, NTHR)),
                       thr[:, i * NTHR:(i + 1) * NTHR].rearrange("p (b j) -> p b j", b=1).to_broadcast((P, GB, NTHR)),
                       op).then_inc(route_op, 1)
                dve.wait_ge(route_op, base + 3)
                nc.vector.tensor_reduce(rt[:, :, 94], rt[:, :, 0:2 * NTHR], AX.X, ALU.add).then_inc(route_op, 1)
                dve.wait_ge(route_op, base + 4)
                tt(rt[:, :, 40:88], rt[:, :, 94:95].to_broadcast((P, GB, 48)),
                   classes[:].rearrange("p (b j) -> p b j", b=1).to_broadcast((P, GB, 48)),
                   ALU.is_equal).then_inc(route_op, 1)
                dve.wait_ge(route_op, base + 5)
                nc.vector.tensor_reduce(ohf[:], rt[:, :, 40:88].rearrange("p b (e k) -> p b e k", e=E_N), AX.X,
                                        ALU.add).then_inc(route_op, 1)
                dve.wait_ge(route_op, base + 6)
                nc.vector.tensor_copy(oh[par][:], ohf[:]).then_inc(oh_ready, 1)

            def route_place(g, par):
                o = ps_a[:, 0:(GB + 1) * E_N].rearrange("p (t e) -> p t e", e=E_N)
                base = 5 * g
                dve.wait_ge(rank_ready, g + 1)
                old = place[1 - par]
                tt(at[:], o[:, 0:GB, :], old[:].rearrange("p (b e) -> p b e", b=1).to_broadcast((P, GB, E_N)),
                   ALU.add).then_inc(place_op, 1)
                tt(place[par][:], o[:, GB, :], old[:], ALU.add).then_inc(place_read, 1)
                dve.wait_ge(place_op, base + 1)
                tt(at2[:], at[:], ohf[:], ALU.mult).then_inc(place_op, 1)
                dve.wait_ge(place_op, base + 2)
                nc.vector.tensor_reduce(rowf[:], at2[:], AX.X, ALU.add).then_inc(place_op, 1)
                ts(tok[par][:], tok[1 - par][:], float(GT), None, ALU.add).then_inc(place_op, 1)
                dve.wait_ge(place_op, base + 4)
                nc.vector.tensor_copy(xr[par][:, :, 2 * D].bitcast(I32), tok[par][:]).then_inc(place_op, 1)
                dve.wait_ge(place_op, base + 5)
                nc.vector.tensor_copy(rowi[par][:], rowf[:]).then_inc(rowi_ready, 1)

            def rotate(g, i, half):
                dve.wait_ge(proj_ready, 4 * g + 2 * i + half + 1)
                if half == 0 and not (known(g) and g == 0 and i == 0):
                    dve.wait_ge(rot_ready, 2 * g + i)
                dst, tab, done = ((rot1, cosT, cos_done), (rot2, sinT, sin_done))[half]
                nc.vector.scalar_tensor_tensor(dst[:], ps_a[:].rearrange("p (b l) -> p b l", b=GB),
                                               bcol[:, 2 * i + half:2 * i + half + 1],
                                               tab[:].rearrange("p (b l) -> p b l", b=1).to_broadcast((P, GB, L)),
                                               ALU.add, ALU.mult).then_inc(done, 1)

            def keep_v(g, par):
                dve.wait_ge(vproj_ready, g + 1)
                if not (known(g) and g < 2):
                    dve.wait_ge(pv_done, GB * (g - 1) + 1)
                tt(vaug[par][:, :, :, 0:DH], ps_a[:].rearrange("p (b h d) -> p b h d", b=GB, h=H),
                   bvr[:].rearrange("p (b h d) -> p b h d", b=1, h=H).to_broadcast((P, GB, H, DH)),
                   ALU.add).then_inc(v_ready, 1)

            def maxima(m, k):
                for u in range(UNITS):
                    dve.wait_ge(s_ready, UNITS * m + u + 1)
                    nc.vector.tensor_reduce(nmax[k % 2][:, u * UH:(u + 1) * UH],
                                            ps_s[:, u % 2, :].rearrange("p (h l) -> p h l", h=UH),
                                            AX.X, ALU.max, negate=True).then_inc(max_done, 1)

            def split_maxima(m, k):
                dve.wait_ge(nmT_ready, m + 1)
                if not (known(m) and m < 2):
                    dve.wait_ge(nm_rows, 32 * (m - 1))
                nc.vector.tensor_copy(nmh[k % 2][:, 0, :], ps_m[0:H, 0:L]).then_inc(nm0_ready, 1)
                dve.wait_ge(nm0_ready, m + 1)
                tt(nmh[k % 2][:, 1, :], ps_m[0:H, 0:L], nmh[k % 2][:, 0, :], ALU.subtract).then_inc(nm_split, 1)

            def normalise(t, k):
                dve.wait_ge(o_ready, t + 1)
                ov = ps_tt[:].rearrange("p u (j w) -> p (u j) w", j=UH)
                nc.vector.reciprocal(rden[k % 2][:], ov[:, :, DH]).then_inc(rden_ready, 1)
                dve.wait_ge(rden_ready, t + 1)
                tt(attn[k % 2][:], ov[:, :, 0:DH],
                   rden[k % 2][:].rearrange("p (h d) -> p h d", d=1).to_broadcast((P, H, DH)),
                   ALU.mult).then_inc(attn_ready, 1)

            def residual(t, k):
                b, par = k % GB, k // GB
                dve.wait_ge(xb_ready, t // GB + 1 if known(t) else (t - b) // GB + 1)
                if b == 0 and not (known(t) and t < CYCLE):
                    dve.wait_ge(rows_out, 16 * (t - GB))
                dve.wait_ge(y_ready, t + 1)
                tt(xr[par][:, b, 0:D], xb[par][:, b, :], ps_m[:, 256:384], ALU.add).then_inc(res_done, 1)

            dve.wait_ge(w_in, 16 * W_IN)
            dve.wait_ge(route_in, 16 * ROUTE_IN)
            dve.wait_ge(consts, 10)
            norm_x(0, 0)
            rotate(0, 0, 0)
            rotate(0, 0, 1)
            rotate(0, 1, 0)
            rotate(0, 1, 1)
            keep_v(0, 0)
            maxima(0, 0)
            split_maxima(0, 0)

            def step(n, k, r, g):
                par = (k // GB + 1) % 2
                b = k % GB
                more = not (known(n) and n == B - 1)
                tail = not (known(n) and n == 0)
                if more:
                    maxima(n + 1, (k + 1) % CYCLE)
                if tail:
                    normalise(n - 1, (k - 1) % CYCLE)
                if more:
                    split_maxima(n + 1, (k + 1) % CYCLE)
                if g is not None and b < 2:
                    rotate(g, b, 0)
                if g is not None and b < 2:
                    rotate(g, b, 1)
                if tail:
                    residual(n - 1, (k - 1) % CYCLE)
                if g is not None and b == 0:
                    norm_x(g, par)
                if g is not None and b == 1:
                    keep_v(g, par)
                if r is not None and b == 1:
                    route_stats(r, par)
                if r is not None and b == 3:
                    route_class(r, par)
                    route_place(r, par)

            run_steps(dve, step)
            normalise(B - 1, CYCLE - 1)
            residual(B - 1, CYCLE - 1)
            last = (NG - 1) % 2
            route_stats(NG - 1, last)
            route_class(NG - 1, last)
            route_place(NG - 1, last)

            done = [0]

            def link(i):
                done[0] += 1
                i.then_inc(table_op, 1)
                dve.wait_ge(table_op, done[0])

            dve.wait_ge(place_read, NG)
            link(ts(padf[:], place[last][:], lane[:, 0:1], None, ALU.add))
            nc.vector.tensor_copy(padi[:], padf[:]).then_inc(pad_ready, 1)
            link(tt(cnt[:], place[last][:], place0[:], ALU.subtract))
            v = big_a[:, 0:E_N * 32].rearrange("p (e k) -> p e k", e=E_N)
            link(tt(v, cnt[:].rearrange("p (e k) -> p e k", k=1).to_broadcast((P, E_N, 32)),
                    k128[:].rearrange("p (e k) -> p e k", e=1).to_broadcast((P, E_N, 32)), ALU.is_gt))
            link(nc.vector.tensor_reduce(tiles_of[:], v, AX.X, ALU.add))
            v = big_b[:, 0:E_N * E_N].rearrange("p (e k) -> p e k", e=E_N)
            link(tt(v, lower[:], tiles_of[:].rearrange("p (e k) -> p e k", e=1).to_broadcast((P, E_N, E_N)), ALU.mult))
            link(nc.vector.tensor_reduce(upto[:], v, AX.X, ALU.add))
            v = big_a[:].rearrange("p (j e) -> p j e", e=E_N)
            w = big_b[:].rearrange("p (j e) -> p j e", e=E_N)
            link(tt(v, upto[:].rearrange("p (j e) -> p j e", j=1).to_broadcast((P, NT, E_N)),
                    tile_no[:].rearrange("p (j e) -> p j e", e=1).to_broadcast((P, NT, E_N)), ALU.is_le))
            link(nc.vector.tensor_reduce(tcls[:], v, AX.X, ALU.add))
            link(tt(w, v, tiles_of[:].rearrange("p (j e) -> p j e", j=1).to_broadcast((P, NT, E_N)), ALU.mult))
            link(nc.vector.tensor_reduce(tbef[:], w, AX.X, ALU.add))
            link(tt(tbef[:], tile_no[:], tbef[:], ALU.subtract))
            link(ts(tbef[:], tbef[:], float(P), None, ALU.mult))
            link(nc.vector.scalar_tensor_tensor(trow[:], tcls[:], float(REGION), tbef[:], ALU.mult, ALU.add))
            link(ts(trow[:], trow[:], float(E_N * REGION), None, ALU.min))
            link(ts(tcls[:], tcls[:], float(E_N - 1), None, ALU.min))
            link(nc.vector.tensor_copy(trow_i[:], trow[:]))
            nc.vector.tensor_copy(tcls_i[:], tcls[:]).then_inc(table_ready, 1)
            dve.wait_ge(ffn_in, 16 * 8)
            link(tt(b2h[:], b2r[:, 0:E_N, :], b2r[:, 1:E_N + 1, :], ALU.add))
            link(ts(b2h[:], b2h[:], 0.5, None, ALU.mult))

            def stage_w1(j, r):
                cls = dve.value_load(tcls_i[0:1, bass.ds(j, 1)], min_val=0, max_val=E_N - 1)
                if not (known(j) and j < 2):
                    dve.wait_ge(h1_ready, j - 1)
                    dve.wait_ge(relu0, j - 1)
                    dve.wait_ge(relu1, j - 1)
                nc.vector.tensor_copy(w1s[r % 2], w1[:, bass.ds(cls, 2), :]).then_inc(w1_staged, 1)
                dve.wait_ge(tile_in[r], laps(j, r) + 16)
                tt(xt[r][:, 0:D], xt[r][:, 0:D], b2h[:, bass.ds(cls, 1), :].rearrange("p e d -> p (e d)"),
                   ALU.add).then_inc(b2_added, 1)

            def relu(j, r):
                dve.wait_ge(h1_ready, j + 1)
                dve.wait_ge(w1_staged, j + 1)
                if not (known(j) and j == 0):
                    dve.wait_ge(y2_ready, j)
                for c in range(FC):
                    i = ts(hid[r % 2][1][:, c, :], (ps_s, ps_t)[r % 2][:, 1, c * P:(c + 1) * P],
                           w1s[r % 2][:, 1, DFF + c:DFF + c + 1], 0.0, ALU.add, ALU.max)
                i.then_inc(relu1, 1)

            def finish(j, r):
                dve.wait_ge(b2_added, j + 1)
                dve.wait_ge(y2_ready, j + 2)
                nc.vector.scalar_tensor_tensor(xt[r][:, 0:D], (ps_o, ps_tt)[r % 2][:, 0, :], 0.5, xt[r][:, 0:D],
                                               ALU.mult, ALU.add).then_inc(fin_done, 1)

            dve.sem_inc(fin_done, 2)
            dve.wait_ge(table_ready, 1)
            dve.wait_ge(pv_done, B + 1)
            stage_w1(0, 0)
            stage_w1(1, 1)
            relu(0, 0)

            def tile(j, r):
                if not (known(j) and j + 1 >= NT):
                    stage_w1(j + 1, (r + 1) % RING)
                relu(j, r)
                finish(j - 1, (r - 1) % RING)

            run_tiles(dve, tile)
            finish(NT - 1, (NT - 1) % RING)


W_IN = 14
ROUTE_IN = 12
_INS = ["x", "ctx_1024", "L0_xattn_bv", "L0_xattn_bo", "L0_ffn_W1", "L0_ffn_W2", "L0_ffn_b2"]


def kernel(**inputs):
    import concourse.bacc as bacc
    from concourse.bass_utils import run_bass_kernel_spmd

    nc = bacc.Bacc("TRN2", target_bir_lowering=False, num_devices=1)
    c = np.ascontiguousarray
    arrays = {n: c(inputs[n]) for n in _INS}
    swap = np.arange(D).reshape(D // 2, 2)[:, ::-1].reshape(D)
    for n in "kq":
        w = np.asarray(inputs[f"L0_xattn_W{n}"])
        arrays[f"W{n}T"] = c(w.T)
        arrays[f"W{n}sT"] = c(w[swap].T)
    for n in "vo":
        arrays[f"W{n}T"] = c(np.asarray(inputs[f"L0_xattn_W{n}"]).T)
    bk, bq = (np.asarray(inputs[f"L0_xattn_b{n}"]) for n in "kq")
    arrays["bcol"] = c(np.stack([bk, bk[swap], bq, bq[swap]], axis=1))
    arrays["b1c"] = c(np.asarray(inputs["L0_ffn_b1"]).reshape(E_N, FC, P).transpose(2, 0, 1))
    half = D // 2
    theta = np.float32(1250) ** (-np.arange(half, dtype=np.float32) / np.float32(half))
    ang = np.arange(L, dtype=np.float32)[:, None] * theta
    arrays["cosT"] = c(np.repeat(np.cos(ang), 2, axis=1).T.astype(np.float32))
    arrays["sinT"] = c(np.stack([-np.sin(ang), np.sin(ang)], axis=2).reshape(L, D).T.astype(np.float32))
    bf = mybir.dt.np(BF16)
    arrays["ident"] = np.eye(P, dtype=np.float32)
    arrays["bigI"] = (np.eye(P) * BIG).astype(bf)
    arrays["maskr"] = c(np.broadcast_to((np.triu(np.ones((L, L)), 1) * -BIG)[:, None, :], (P, UH, L)).astype(bf))
    j = np.arange(1, NTHR + 1, dtype=np.float32)
    f32 = np.float32
    arrays["thr"] = np.concatenate([j, -j])[None, :]
    arrays["classes"] = (NTHR + np.arange(E_N)[:, None] + 8 * (np.arange(6)[None, :] - 3)).astype(f32).reshape(1, 48)
    arrays["place0"] = (np.arange(E_N, dtype=f32) * REGION)[None, :]
    arrays["k128"] = (np.arange(32, dtype=f32) * P)[None, :]
    arrays["tile_no"] = np.arange(NT, dtype=f32)[None, :]
    arrays["lower"] = np.tril(np.ones((E_N, E_N), f32))[None]
    arrays["tri"] = np.triu(np.ones((P, P), f32), 1).astype(bf)
    arrays["ones"] = np.ones((P, P), f32).astype(bf)
    arrays["lane"] = np.arange(P, dtype=f32)[:, None]
    arrays["tok"] = (np.arange(P)[:, None] + P * np.arange(GB)[None, :] - GT).astype(f32)
    arrays["pad"] = np.zeros((P, XW), f32)
    arrays["pad"][:, 2 * D] = (TOK + np.arange(P, dtype=np.int32)).view(f32)
    aps = {n: nc.dram_tensor(f"in_{n}", v.shape, mybir.dt.from_np(v.dtype), kind="ExternalInput").ap()
           for n, v in arrays.items()}
    out = nc.dram_tensor("out_0", (B, L, D), F32, kind="ExternalOutput").ap()
    build(nc, aps, out)
    r = run_bass_kernel_spmd(nc, [{f"in_{n}": v for n, v in arrays.items()}], core_ids=[0])
    return r.results[0]["out_0"]
```

```python
from contextlib import ExitStack

import numpy as np

import concourse.bass as bass
from concourse import mybir

F32 = mybir.dt.float32
BF16 = mybir.dt.bfloat16
I32 = mybir.dt.int32
U32 = mybir.dt.uint32
ALU = mybir.AluOpType
ACT = mybir.ActivationFunctionType
AX = mybir.AxisListType

P = 128
B, L, D = 32, 128, 128
H, DH = 16, 8
HP = H // 2
GB = 4
NG = B // GB
GT = GB * L
UNITS = 4
UH = H // UNITS
PARTS = 3
Q_PART = (0, 1, 2, 0, 1, 0)
K_PART = (0, 0, 0, 1, 1, 2)
SLOTS = len(Q_PART)
HROWS = SLOTS * DH
PROWS = 2 * HROWS
MROWS = PROWS + 2
VW = 32
E_N, DFF = 8, 512
FC = DFF // P
EPS = 1e-5
SCALE = DH ** -0.5
BIG = 2.0 ** 15
CYCLE = 2 * GB
FIRST = GB + 2
LAST = GB
TOK = B * L
REGION = TOK + P
NT = (TOK + (E_N - 1) * (P - 1)) // P + 1
XW = 2 * D + 1
LEAD = 7
RING = 6
NTHR = 17
ROW_CONSTS = (2 * NTHR, 6 * E_N, E_N, 32, NT, E_N * E_N)


def build(nc, a, out):
    with ExitStack() as ctx:
        def sb(name, shape, dt=F32):
            return ctx.enter_context(nc.sbuf_tensor(name, shape, dt))

        def ps(name, shape):
            return ctx.enter_context(nc.psum_tensor(name, shape, F32))

        def sem(name):
            return ctx.enter_context(nc.semaphore(name))

        q_rows = nc.dram_tensor("q_rows", [H, DH, SLOTS, GT], BF16, kind="Internal").ap()
        rows = nc.dram_tensor("rows", [E_N * REGION + P, XW], F32, kind="Internal").ap()
        k_rows = nc.dram_tensor("k_rows", [H, DH, SLOTS, GT], BF16, kind="Internal").ap()

        w_first = sb("w_first", [P, 5, D])
        w_rest = sb("w_rest", [P, 4, D])
        masks = sb("masks", [P, 3 + UH, P], BF16)
        cols = sb("cols", [P, 4 + 1 + GB + XW])
        row_consts = sb("row_consts", [P, 2 * D + sum(ROW_CONSTS)])
        xin = [sb(f"xin{i}", [P, GB, D]) for i in range(2)]
        xb = [sb(f"xb{i}", [P, GB, D]) for i in range(2)]
        xr = [sb(f"xr{i}", [P, GB, XW]) for i in range(2)]
        ctxb = [sb(f"ctxb{i}", [P, GB, D]) for i in range(2)]
        xn = [sb(f"xn{i}", [P, GB, D]) for i in range(2)]
        xT = sb("xT", [P, GT])
        cT = sb("cT", [P, GT])
        rot1 = sb("rot1", [P, GB, L])
        rot2 = sb("rot2", [P, GB, L])
        rot = [sb(f"rot{i}", [P, GT]) for i in "kq"]
        rest = sb("rest", [P, GT])
        parts = [sb(f"parts_{i}", [P, PARTS, GT], BF16) for i in "kq"]
        qst = [sb(f"qst{i}", [P, HP, 2, GT], BF16) for i in range(2)]
        kst = [sb(f"kst{i}", [P, HP, GT], BF16) for i in range(2)]
        vaug = [sb(f"vaug{i}", [P, GB, H, VW]) for i in range(2)]
        ex = [sb(f"ex{i}", [P, H, L]) for i in range(2)]
        oT = sb("oT", [P, UNITS, L])
        attn = [sb(f"attn{i}", [P, H, DH]) for i in range(2)]
        attnT = sb("attnT", [P, L])
        nmax = [sb(f"nmax{i}", [P, H]) for i in range(2)]
        nmh = [sb(f"nmh{i}", [H, 2, L], BF16) for i in range(2)]
        rden = [sb(f"rden{i}", [P, H]) for i in range(2)]
        stats = sb("stats", [P, GB, 6])
        lnb = sb("lnb", [P, 8, GB])
        stats2 = sb("stats2", [P, GB, 6])
        ln2b = sb("ln2b", [P, 8, GB])
        gate = sb("gate", [P, 2 * CYCLE + 2 + RING])
        ident, wk, wks, cosT, sinT = (w_first[:, i, :] for i in range(5))
        wq, wqs, wv, wo = (w_rest[:, i, :] for i in range(4))
        bigI, tri, ones = (masks[:, i, :] for i in range(3))
        maskr = masks[:, 3:3 + UH, :]
        bcol = cols[:, 0:4]
        lane = cols[:, 4:5]
        tok_first = cols[:, 5:5 + GB]
        pad = cols[:, 5 + GB:5 + GB + XW]
        bvr, bor = row_consts[:, 0:D], row_consts[:, D:2 * D]
        at0 = [2 * D + sum(ROW_CONSTS[:i]) for i in range(7)]
        thr, classes, place0, k128, tile_no, lower = (row_consts[:, at0[i]:at0[i + 1]] for i in range(6))
        lower = lower.rearrange("p (e k) -> p e k", e=E_N)
        w1 = sb("w1", [P, E_N + 1, DFF + FC])
        w2 = sb("w2", [P, E_N + 1, FC, D])
        b2r = sb("b2r", [P, E_N + 1, D])
        b2h = sb("b2h", [P, E_N, D])
        rt = sb("rt", [P, GB, 96])
        oh = [sb(f"oh{i}", [P, GB, E_N], BF16) for i in range(2)]
        ohf = sb("ohf", [P, GB, E_N])
        place = [sb(f"place{i}", [P, E_N]) for i in range(2)]
        at = sb("at", [P, GB, E_N])
        at2 = sb("at2", [P, GB, E_N])
        rowf = sb("rowf", [P, GB])
        rowi = [sb(f"rowi{i}", [P, GB], I32) for i in range(2)]
        tok = [sb("tok0", [P, GB]), tok_first]
        padi = sb("padi", [P, E_N], I32)
        cnt = sb("cnt", [P, E_N])
        big_a = sb("big_a", [P, NT * E_N])
        big_b = sb("big_b", [P, NT * E_N])
        tiles_of = sb("tiles_of", [P, E_N])
        upto = sb("upto", [P, E_N])
        tcls = sb("tcls", [P, NT])
        tbef = sb("tbef", [P, NT])
        trow = sb("trow", [P, NT])
        tcls_i = sb("tcls_i", [P, NT], I32)
        trow_i = sb("trow_i", [P, NT], I32)
        xt = [qst[0][:, i, :, :].rearrange("p a t -> p (a t)").bitcast(F32)[:, 0:XW] for i in range(RING)]
        w1s = [ex[i][:].rearrange("p h l -> p (h l)")[:, 0:2 * (DFF + FC)].rearrange("p (e f) -> p e f", e=2)
               for i in range(2)]
        hid = [[kst[i][:, 2 * e:2 * e + 2, :].rearrange("p a t -> p (a t)").bitcast(F32)
                .rearrange("p (c t) -> p c t", c=FC) for e in range(2)] for i in range(2)]
        xtT = [xn[i][:, 0, :] for i in range(2)]

        ps_s = ps("ps_s", [P, 2, UH * L])
        ps_t = ps("ps_t", [P, 2, UH * L])
        ps_o = ps("ps_o", [P, UNITS, L])
        ps_tt = ps("ps_tt", [P, UNITS, P])
        ps_a = ps("ps_a", [P, GT])
        ps_m = ps("ps_m", [P, 512])

        def bank(g, what):
            if known(g) and g == 0:
                return {"k": ps_s[:, 0, :], "k swapped": ps_s[:, 1, :], "q": ps_t[:, 0, :], "q swapped": ps_t[:, 1, :],
                        "v": ps_o[:].rearrange("p u l -> p (u l)"), "xT": ps_m[:], "ctxT": ps_a[:]}[what]
            return ps_a[:]

        KINDS = ("k", "k swapped", "q", "q swapped")

        x_in = [sem(f"x_in{i}") for i in range(2)]
        ffn_in = sem("ffn_in")
        w_rest_in = sem("w_rest_in")
        place_read = sem("place_read")
        xb_ready = sem("xb_ready")
        w_in = sem("w_in")
        ctx_in = [sem(f"ctx_in{i}") for i in range(2)]
        set_by_pool = sem("set_by_pool")
        set_by_dve = sem("set_by_dve")
        var_ready = sem("var_ready")
        rstd_ready = sem("rstd_ready")
        ln_op = sem("ln_op")
        xn_ready = sem("xn_ready")
        x_mean_off = sem("x_mean_off")
        x2_mean_off = sem("x2_mean_off")
        ctxT_ready = sem("ctxT_ready")
        ctxT_in_sb = sem("ctxT_in_sb")
        xT_ready = sem("xT_ready")
        xT_in_sb = sem("xT_in_sb")
        proj_ready = sem("proj_ready")
        cos_done = sem("cos_done")
        sin_done = sem("sin_done")
        rot_ready = sem("rot_ready")
        part0_ready = sem("part0_ready")
        rest_ready = sem("rest_ready")
        part1_ready = sem("part1_ready")
        part2_ready = sem("part2_ready")
        vproj_ready = sem("vproj_ready")
        v_ready = sem("v_ready")
        k_out = sem("k_out")
        q_out = sem("q_out")
        stacks_in = sem("stacks_in")
        s_ready = sem("s_ready")
        max_done = sem("max_done")
        nmT_ready = sem("nmT_ready")
        nm0_ready = sem("nm0_ready")
        nm_split = sem("nm_split")
        nm_rows = sem("nm_rows")
        st_ready = sem("st_ready")
        exp_done = sem("exp_done")
        mask_done = sem("mask_done")
        pv_done = sem("pv_done")
        oT_in_sb = sem("oT_in_sb")
        o_ready = sem("o_ready")
        rden_ready = sem("rden_ready")
        attn_ready = sem("attn_ready")
        attnT_ready = sem("attnT_ready")
        attnT_in_sb = sem("attnT_in_sb")
        y_ready = sem("y_ready")
        res_done = sem("res_done")
        ln2_op = sem("ln2_op")
        var2_ready = sem("var2_ready")
        rstd2_ready = sem("rstd2_ready")
        xn2_ready = sem("xn2_ready")
        route_op = sem("route_op")
        oh_ready = sem("oh_ready")
        rank_ready = sem("rank_ready")
        place_op = sem("place_op")
        rowi_ready = sem("rowi_ready")
        rows_out = sem("rows_out")
        pads_out = sem("pads_out")
        spare_out = sem("spare_out")
        table_op = sem("table_op")
        pad_ready = sem("pad_ready")
        table_ready = sem("table_ready")
        tile_in = [sem(f"tile_in{i}") for i in range(RING)]
        w1_staged = sem("w1_staged")
        b2_added = sem("b2_added")
        xt_T_ready = sem("xt_T_ready")
        xt_T_in_sb = sem("xt_T_in_sb")
        h0_ready = sem("h0_ready")
        h1_ready = sem("h1_ready")
        relu0 = sem("relu0")
        relu1 = sem("relu1")
        y2_ready = sem("y2_ready")
        fin_done = sem("fin_done")
        gate_passed = sem("gate_passed")
        out_stored = [sem(f"out_stored{i}") for i in range(RING)]

        block = ctx.enter_context(nc.Block())

        def run_steps(eng, step):
            def alone(n):
                step(n, n % CYCLE, lambda d: n // GB + d if 0 <= n // GB + d < NG else None)

            for n in range(FIRST):
                alone(n)
            whole = (B - FIRST - LAST) // CYCLE
            with eng.Fori(0, whole) as c:
                for k in range(FIRST, FIRST + CYCLE):
                    step(c * CYCLE + k, k % CYCLE, lambda d: c * 2 + (k // GB + d))
            for n in range(FIRST + whole * CYCLE, B):
                alone(n)

        def run_tiles(eng, tile):
            whole = (NT - RING) // RING
            with eng.Fori(0, whole) as q:
                for k in range(1, RING + 1):
                    tile(q * RING + k, k % RING, lambda d: q * 16 + 16 * ((k + d) // RING))
            for j in range(whole * RING + 1, NT):
                tile(j, j % RING, lambda d: 16 * ((j + d) // RING))

        def blank(t):
            return t[:].rearrange("p g m t -> p (g m t)").bitcast(F32)

        def write_pads(eng, classes_of):
            for e in classes_of:
                row = eng.value_load(padi[0:1, e:e + 1], min_val=e * REGION, max_val=e * REGION + TOK)
                eng.dma_start(rows[bass.ds(row, P), :], pad).then_inc(pads_out, 16)

        def known(n):
            return isinstance(n, int)

        @block.sync
        def _(sp):
            xv = a["x"].rearrange("b l d -> l b d")
            cv = a["ctx_1024"].rearrange("b l d -> l b d")

            def load_ctx(g, par):
                sp.dma_start(ctxb[par][:], cv[:, bass.ts(g, GB), :]).then_inc(ctx_in[par], 16)

            def load_x(g, par):
                sp.dma_start(xin[par][:], xv[:, bass.ts(g, GB), :]).then_inc(x_in[par], 16)

            load_ctx(0, 0)
            sp.dma_start(w_first[:], a["w_first"]).then_inc(w_in, 16)
            load_x(0, 0)
            sp.dma_start(cols[:], a["cols"]).then_inc(w_in, 16)
            sp.dma_start(w_rest[:], a["w_rest"]).then_inc(w_rest_in, 16)
            sp.dma_start(row_consts[:], a["row_consts"].to_broadcast((P, 2 * D + sum(ROW_CONSTS)))).then_inc(w_rest_in, 16)
            sp.dma_start(masks[:], a["masks"]).then_inc(w_rest_in, 16)
            load_ctx(1, 1)
            load_x(1, 1)

            def load_w1(e0, e1, of):
                sp.dma_start(w1[:, e0:e1, 0:DFF],
                             a["L0_ffn_W1"][of:of + e1 - e0].rearrange("e d f -> d e f")).then_inc(ffn_in, 16)

            def load_w2(e0, e1, of):
                sp.dma_start(w2[:, e0:e1],
                             a["L0_ffn_W2"][of:of + e1 - e0].rearrange("e (c p) d -> p e c d", p=P)).then_inc(ffn_in, 16)

            def load_ffn(n):
                if n == 0:
                    load_w1(E_N, E_N + 1, 0)
                    sp.dma_start(w1[:, :, DFF:DFF + FC], a["b1c"]).then_inc(ffn_in, 16)
                if n == 1:
                    load_w2(E_N, E_N + 1, 0)
                    sp.dma_start(b2r[:], a["b2"].to_broadcast((P, E_N + 1, D))).then_inc(ffn_in, 16)
                i = n - (B - E_N - 2)
                if 0 <= i < E_N:
                    (load_w1, load_w2)[i % 2](i // 2 * 2, i // 2 * 2 + 2, i // 2 * 2)

            sp.wait_ge(w_in, 32)
            sp.dma_start(rows[E_N * REGION:E_N * REGION + P, :], pad[:]).then_inc(spare_out, 16)

            def k_write(g):
                if not (known(g) and g == 0):
                    sp.wait_ge(stacks_in, 64 * g)
                sp.wait_ge(part2_ready, 2 * g + 1)
                to = k_rows.rearrange("h r s t -> (h r) s t")
                for s, w in ((0, 3), (3, 2), (5, 1)):
                    sp.dma_start(to[:, s:s + w, :], parts[0][:, K_PART[s]:K_PART[s] + 1, :].to_broadcast((P, w, GT))
                                 ).then_inc(k_out, 16)

            def k_read(g, par, n):
                if not (known(n) and n == 0):
                    sp.wait_ge(exp_done, UNITS * n)
                sp.wait_ge(k_out, 48 * (g + 1) if known(g) else (48 // GB) * n + 96)
                for m in range(2):
                    sp.dma_start(kst[par][m * HROWS:(m + 1) * HROWS, :, :],
                                 k_rows.rearrange("(g m) r s t -> m (r s) g t", m=2)[m]).then_inc(stacks_in, 16)

            def q_write(g):
                sp.wait_ge(part2_ready, 2 * g + 2)
                to = q_rows.rearrange("h r s t -> (h r) s t")
                for s, w in ((0, 3), (3, 2), (5, 1)):
                    sp.dma_start(to[:, s:s + w, :], parts[1][:, 0:w, :]).then_inc(q_out, 16)

            def q_read(g, par):
                sp.wait_ge(q_out, 48 * (g + 1))
                for m in range(2):
                    sp.dma_start(qst[par][m * HROWS:(m + 1) * HROWS, :, m, :],
                                 q_rows.rearrange("(g m) r s t -> m (r s) g t", m=2)[m]).then_inc(stacks_in, 16)

            def maxima_rows(m, k):
                sp.wait_ge(nm_split, m + 1)
                b = k % GB
                for s in range(2):
                    sp.dma_start(qst[k // GB][PROWS + s:PROWS + s + 1, :, :, b * L:(b + 1) * L],
                                 nmh[k % 2][:, s, :]).then_inc(nm_rows, 16)

            k_write(0)
            sp.wait_ge(set_by_dve, 5)
            sp.wait_ge(set_by_pool, 4)
            k_read(0, 0, 0)
            q_write(0)
            q_read(0, 0)
            sp.wait_ge(set_by_pool, 5)
            sp.wait_ge(ctxT_ready, 1)
            load_ctx(2, 0)
            sp.wait_ge(xb_ready, 1)
            load_x(2, 0)
            k_write(1)
            maxima_rows(0, 0)

            def step(n, k, grp):
                b, own = k % GB, k // GB
                if b == 0 and grp(1) is not None:
                    k_read(grp(1), 1 - own, n)
                if b == 3 and grp(3) is not None:
                    sp.wait_ge(ctxT_ready, grp(2))
                    load_ctx(grp(3), 1 - own)
                if not (known(n) and n == B - 1):
                    maxima_rows(n + 1, (k + 1) % CYCLE)
                if b == 1 and grp(1) is not None:
                    q_read(grp(1), 1 - own)
                if b == 3 and grp(3) is not None:
                    sp.wait_ge(xb_ready, grp(2))
                    load_x(grp(3), 1 - own)
                if b == 3 and grp(2) is not None:
                    k_write(grp(2))
                if b == 0 and grp(1) is not None:
                    q_write(grp(1))
                if known(n):
                    load_ffn(n)

            run_steps(sp, step)

            def load_tile(j, r):
                row = sp.value_load(trow_i[0:1, bass.ds(j, 1)], min_val=0, max_val=E_N * REGION)
                sp.dma_start(xt[r], rows[bass.ds(row, P), :]).then_inc(tile_in[r], 16)

            sp.wait_ge(pad_ready, 1)
            write_pads(sp, range(E_N // 2))
            sp.wait_ge(table_ready, 1)
            sp.wait_ge(rows_out, 16 * B)
            sp.wait_ge(spare_out, 16)
            sp.wait_ge(pads_out, 16 * E_N)
            for j in range(RING):
                load_tile(j, j)

            def tile(j, r, lap):
                if known(j) and j + RING - 1 >= NT:
                    return
                sp.wait_ge(out_stored[(r - 1) % RING], lap(RING - 1))
                load_tile(j + RING - 1, (r - 1) % RING)

            run_tiles(sp, tile)
            for r in range(RING):
                sp.wait_ge(out_stored[r], 16 * ((NT - 1 - r) // RING + 1))

        @block.gpsimd
        def _(pool):
            nc.gpsimd.memset(lnb[:, 7, :], -0.5).then_inc(set_by_pool, 1)
            nc.gpsimd.memset(gate[:], 0.0).then_inc(set_by_pool, 1)
            nc.gpsimd.memset(blank(qst[0]), 0.0).then_inc(set_by_pool, 1)

            def pass_gate(j):
                return nc.gpsimd.tensor_tensor(gate[:, j:j + 1], lnb[:, 7, 0:1], lnb[:, 7, 0:1], ALU.add)

            def rstd2(g):
                pool.wait_ge(var2_ready, g + 1)
                nc.gpsimd.tensor_tensor(ln2b[:, 6, :], ln2b[:, 5, :], lnb[:, 7, :], ALU.pow).then_inc(rstd2_ready, 1)

            def scatter(g, par, t):
                if t == 0:
                    pool.wait_ge(rowi_ready, g + 1)
                    pass_gate(2 * CYCLE + par)
                nc.gpsimd.indirect_dma_start(rows, bass.IndirectOffsetOnAxis(ap=rowi[par][:, t:t + 1], axis=0),
                                             xr[par][:, t, :], None).then_inc(rows_out, 16)

            def rstd(g):
                pool.wait_ge(var_ready, g + 1)
                nc.gpsimd.tensor_tensor(lnb[:, 6, :], lnb[:, 5, :], lnb[:, 7, :], ALU.pow).then_inc(rstd_ready, 1)

            def take_part0(g, i):
                if not (known(g) and g == 0 and i == 0):
                    pool.wait_ge(part2_ready, 2 * g + i)
                pool.wait_ge(part0_ready, 2 * g + i + 1)
                nc.gpsimd.tensor_tensor(rest[:], rot[i][:], parts[i][:, 0, :], ALU.subtract).then_inc(rest_ready, 1)

            def take_part1(g, i):
                pool.wait_ge(part1_ready, 2 * g + i + 1)
                nc.gpsimd.tensor_tensor(parts[i][:, 2, :], rest[:], parts[i][:, 1, :],
                                        ALU.subtract).then_inc(part2_ready, 1)

            def mask(n, k, u):
                pool.wait_ge(exp_done, UNITS * n + u + 1)
                pass_gate((k * UNITS + u) % (2 * CYCLE))
                e = ex[k % 2][:, u * UH:(u + 1) * UH, :]
                nc.gpsimd.affine_select(out=e, in_=e, pattern=[[0, UH], [1, L]], compare_op=ALU.is_ge, fill=0.0,
                                        base=0, channel_multiplier=-1).then_inc(mask_done, 1)

            pool.wait_ge(set_by_pool, 3)
            rstd(0)
            nc.gpsimd.memset(kst[1][:], 1.0).then_inc(set_by_pool, 1)
            take_part0(0, 0)
            rstd(1)
            take_part1(0, 0)
            take_part0(0, 1)
            take_part1(0, 1)
            nc.gpsimd.memset(blank(qst[1]), 0.0).then_inc(set_by_pool, 1)
            take_part0(1, 0)
            take_part1(1, 0)

            def step(n, k, grp):
                b, own = k % GB, k // GB
                for u in range(UNITS):
                    if b == 1 and u == 2 and grp(2) is not None:
                        rstd(grp(2))
                    mask(n, k, u)
                    if b == 0:
                        if u == 0 and grp(1) is not None:
                            take_part0(grp(1), 1)
                        if u == 2 and grp(1) is not None:
                            take_part1(grp(1), 1)
                        if u == 3 and grp(-2) is not None:
                            scatter(grp(-2), own, 0)
                    if b == 1:
                        if u < 3 and grp(-2) is not None:
                            scatter(grp(-2), own, u + 1)
                    if b == 2:
                        if u == 2 and grp(-1) is not None:
                            rstd2(grp(-1))
                        if u == 3 and grp(2) is not None:
                            take_part0(grp(2), 0)
                    if b == 3 and u == 1 and grp(2) is not None:
                        take_part1(grp(2), 0)

            run_steps(pool, step)
            for t in range(GB):
                scatter(NG - 2, (NG - 2) % 2, t)
            rstd2(NG - 1)
            for t in range(GB):
                scatter(NG - 1, (NG - 1) % 2, t)
            def store(j, r):
                pool.wait_ge(gate_passed, j + 1)
                pool.wait_ge(fin_done, j + 3)
                pass_gate(2 * CYCLE + 2 + r).then_inc(gate_passed, 1)
                nc.gpsimd.indirect_dma_start(out.rearrange("b l d -> (b l) d"),
                                             bass.IndirectOffsetOnAxis(ap=xt[r][:, 2 * D:XW].bitcast(U32), axis=0),
                                             xt[r][:, 0:D], None, bounds_check=TOK - 1,
                                             oob_is_err=False).then_inc(out_stored[r], 16)

            pool.sem_inc(gate_passed, RING)
            run_tiles(pool, lambda j, r, lap: store(j - 1, (r - 1) % RING))
            store(NT - 1, (NT - 1) % RING)

        @block.scalar
        def _(act):
            def evac_ctxT(g):
                act.wait_ge(ctxT_ready, g + 1)
                if known(g) and g == 1:
                    act.wait_ge(vproj_ready, 1)
                nc.scalar.activation(cT[:], bank(g, "ctxT"), ACT.Copy).then_inc(ctxT_in_sb, 1)

            def evac_xT(g):
                act.wait_ge(xT_ready, g + 1)
                nc.scalar.activation(xT[:], bank(g, "xT"), ACT.Copy).then_inc(xT_in_sb, 1)

            def layernorm(of, to, b, mean_off, done, passes):
                for t in range(GB):
                    nc.scalar.activation(to(t), of(t), ACT.Identity, bias=b[:, 0, t:t + 1]).then_inc(mean_off, 1)
                act.wait_ge(mean_off, passes)
                for t in range(GB):
                    nc.scalar.activation(to(t), to(t), ACT.Copy, scale=b[:, 6, t:t + 1]).then_inc(done, 1)

            def norm_x(g, par):
                act.wait_ge(rstd_ready, g + 1)
                layernorm(lambda t: xin[par][:, t, :], lambda t: xn[par][:, t, :], lnb, x_mean_off, xn_ready, GB * (g + 1))

            def route_norm(g, par):
                act.wait_ge(rstd2_ready, g + 1)
                layernorm(lambda t: xr[par][:, t, 0:D], lambda t: xr[par][:, t, D:2 * D], ln2b, x2_mean_off, xn2_ready,
                          GB * (g + 1))

            def part0(g, i):
                if not (known(g) and g == 0):
                    act.wait_ge((k_out, q_out)[i], 48 * g)
                act.wait_ge(rot_ready, 2 * g + i + 1)
                nc.scalar.activation(parts[i][:, 0, :], rot[i][:], ACT.Copy).then_inc(part0_ready, 1)

            def part1(g, i):
                act.wait_ge(rest_ready, 2 * g + i + 1)
                nc.scalar.activation(parts[i][:, 1, :], rest[:], ACT.Copy).then_inc(part1_ready, 1)

            def exp(n, k, u):
                if u == 0 and not (known(n) and n == 0):
                    act.wait_ge(pv_done, n)
                act.wait_ge(st_ready, UNITS * n + u + 1)
                nc.scalar.activation(ex[k % 2][:, u * UH:(u + 1) * UH, :],
                                     ps_t[:, u % 2, :].rearrange("p (h l) -> p h l", h=UH),
                                     ACT.Exp, scale=SCALE).then_inc(exp_done, 1)

            def evac_o(n):
                act.wait_ge(pv_done, n + 2)
                nc.scalar.activation(oT[:], ps_o[:], ACT.Copy).then_inc(oT_in_sb, 1)

            def evac_attnT(t):
                act.wait_ge(attnT_ready, t + 1)
                nc.scalar.activation(attnT[:], ps_tt[:, 0, :], ACT.Copy).then_inc(attnT_in_sb, 1)

            evac_ctxT(0)
            norm_x(0, 0)
            evac_xT(0)
            part0(0, 0)
            part1(0, 0)
            part0(0, 1)
            evac_ctxT(1)
            part1(0, 1)
            norm_x(1, 1)
            evac_xT(1)
            part0(1, 0)
            part1(1, 0)

            def step(n, k, grp):
                b, own = k % GB, k // GB
                for u in range(UNITS):
                    if u == 2 and not (known(n) and n < 1):
                        evac_o(n - 1)
                    exp(n, k, u)
                    if u == 2 and not (known(n) and n < 2):
                        evac_attnT(n - 2)
                    if b == 0 and grp(1) is not None:
                        if u == 0:
                            part0(grp(1), 1)
                        if u == 1:
                            part1(grp(1), 1)
                    if b == 1 and u == 0 and grp(2) is not None:
                        evac_ctxT(grp(2))
                    if b == 1 and u == 3 and grp(2) is not None:
                        norm_x(grp(2), own)
                    if b == 2 and u == 2 and grp(2) is not None:
                        part0(grp(2), 0)
                        evac_xT(grp(2))
                    if b == 2 and u == 3 and grp(-1) is not None:
                        route_norm(grp(-1), 1 - own)
                    if b == 3 and u == 0 and grp(2) is not None:
                        part1(grp(2), 0)

            run_steps(act, step)
            evac_o(B - 1)
            evac_attnT(B - 2)
            evac_attnT(B - 1)

            route_norm(NG - 1, (NG - 1) % 2)
            act.wait_ge(pad_ready, 1)
            write_pads(act, range(E_N // 2, E_N))

            def evac_tile(j, r):
                act.wait_ge(xt_T_ready, j + 1)
                nc.scalar.activation(xtT[r % 2], (ps_a[:, 0:P], ps_m[:, 0:P])[r % 2], ACT.Copy).then_inc(xt_T_in_sb, 1)

            def relu(j, r):
                act.wait_ge(h0_ready, j + 1)
                if not (known(j) and j == 0):
                    act.wait_ge(y2_ready, j)
                for c in range(FC):
                    i = nc.scalar.activation(hid[r % 2][0][:, c, :], (ps_s, ps_t)[r % 2][:, 0, c * P:(c + 1) * P],
                                             ACT.Relu, bias=w1s[r % 2][:, 0, DFF + c:DFF + c + 1])
                i.then_inc(relu0, 1)

            evac_tile(0, 0)
            evac_tile(1, 1)
            relu(0, 0)

            def tile(j, r, lap):
                if not (known(j) and j + 1 >= NT):
                    evac_tile(j + 1, (r + 1) % RING)
                relu(j, r)

            run_tiles(act, tile)

        @block.tensor
        def _(pe):
            mm, tr = nc.tensor.matmul, nc.tensor.transpose
            pe.sem_inc(pv_done, 1)

            def ctx_transpose(g, par):
                pe.wait_ge(ctx_in[par], 8 * (g - par) + 16)
                if known(g) and g == 1:
                    pe.wait_ge(ctxT_in_sb, 1)
                elif not known(g) or g > 1:
                    pe.wait_ge(v_ready, g)
                for t in range(GB):
                    i = tr(bank(g, "ctxT")[:, t * L:(t + 1) * L], ctxb[par][:, t, :], ident[:])
                i.then_inc(ctxT_ready, 1)

            def x_transpose(g, par):
                pe.wait_ge(xn_ready, GB * (g + 1))
                if not (known(g) and g == 0):
                    pe.wait_ge(sin_done, 2 * g + 1)
                for t in range(GB):
                    i = tr(bank(g, "xT")[:, t * L:(t + 1) * L], xn[par][:, t, :], ident[:])
                i.then_inc(xT_ready, 1)

            def project(g, i):
                if i % 2 == 0:
                    pe.wait_ge((ctxT_in_sb, xT_in_sb)[i // 2], g + 1)
                elif not (known(g) and g == 0):
                    pe.wait_ge(cos_done, 2 * g + i // 2 + 1)
                mm(bank(g, KINDS[i]), (wk, wks, wq, wqs)[i][:], (cT, cT, xT, xT)[i][:], start=True,
                   stop=True).then_inc(proj_ready, 1)

            def project_v(g):
                if known(g) and 0 < g < 3:
                    pe.wait_ge(sin_done, 2 * g + 2)
                elif not known(g) or g >= 3:
                    pe.wait_ge(place_read, g - 2)
                for t in range(GB):
                    i = mm(bank(g, "v")[:, t * L:(t + 1) * L], cT[:, t * L:(t + 1) * L], wv[:], start=True, stop=True)
                i.then_inc(vproj_ready, 1)

            def scores(m, k, u):
                b, par = k % GB, k // GB
                tok = slice(b * L, (b + 1) * L)
                if u == 0 and b == 0:
                    pe.wait_ge(stacks_in, 16 * m + 64)
                if not (known(m) and m * UNITS + u < 2):
                    pe.wait_ge(max_done, UNITS * m + u - 1)
                bank = ps_s[:, u % 2, :]
                mm(bank, bigI[:], maskr[:].rearrange("p h l -> p (h l)"), start=True, stop=False, skip_group_check=True)
                for j in range(UH):
                    h = u * UH + j
                    i = mm(bank[:, j * L:(j + 1) * L], qst[par][0:PROWS, h // 2, h % 2, tok],
                           kst[par][0:PROWS, h // 2, tok], start=False, stop=(j == UH - 1), skip_group_check=True)
                i.then_inc(s_ready, 1)

            def maxima_transpose(m, k):
                pe.wait_ge(max_done, UNITS * (m + 1))
                if not (known(m) and m == 0):
                    pe.wait_ge(nm_split, m)
                if not (known(m) and m < 3):
                    pe.wait_ge(res_done, m - 2)
                tr(ps_m[0:H, 0:L], nmax[k % 2][:], ident[:]).then_inc(nmT_ready, 1)

            def scores_t(n, k, u):
                b, par = k % GB, k // GB
                tok = slice(b * L, (b + 1) * L)
                if u == 0:
                    pe.wait_ge(nm_rows, 32 * (n + 1))
                if not (known(n) and n * UNITS + u < 2):
                    pe.wait_ge(exp_done, UNITS * n + u - 1)
                for j in range(2):
                    g = 2 * u + j
                    i = mm(ps_t[:, u % 2, j * 2 * L:(j + 1) * 2 * L], kst[par][0:MROWS, g, tok],
                           qst[par][0:MROWS, g, :, tok], start=True, stop=True)
                i.then_inc(st_ready, 1)

            def weigh_v(n, k, u):
                b, par = k % GB, k // GB
                if u == 0:
                    pe.wait_ge(v_ready, n // GB + 1 if known(n) else (n - b) // GB + 1)
                    if not (known(n) and n == 0):
                        pe.wait_ge(oT_in_sb, n)
                pe.wait_ge(mask_done, UNITS * n + u + 1)
                for j in range(UH):
                    h = u * UH + j
                    i = mm(ps_o[j * VW:(j + 1) * VW, u, :], vaug[par][:, b, h, :], ex[k % 2][:, h, :], start=True, stop=True)
                if u == UNITS - 1:
                    i.then_inc(pv_done, 1)

            def o_transpose(t):
                pe.wait_ge(oT_in_sb, t + 1)
                if not (known(t) and t == 0):
                    pe.wait_ge(attnT_in_sb, t)
                for u in range(UNITS):
                    i = tr(ps_tt[:, u, :], oT[:, u, :], ident[:])
                i.then_inc(o_ready, 1)

            def attn_transpose(t, k):
                pe.wait_ge(attn_ready, t + 1)
                tr(ps_tt[:, 0, :], attn[k % 2][:].rearrange("p h d -> p (h d)"), ident[:]).then_inc(attnT_ready, 1)

            def project_o(t):
                pe.wait_ge(attnT_in_sb, t + 1)
                if known(t) and t + 3 >= B:
                    pe.wait_ge(res_done, t + 1)
                else:
                    pe.wait_ge(nm_split, t + 4)
                mm(ps_m[:, 128:256], attnT[:], wo[:], start=True, stop=True).then_inc(y_ready, 1)

            def ranks(g, par):
                pe.wait_ge(oh_ready, g + 1)
                if known(g) and g + 3 > NG:
                    pe.wait_ge(place_read, g)
                elif known(g) and g + 3 == NG:
                    pe.wait_ge(v_ready, NG)
                else:
                    pe.wait_ge(sin_done, 2 * g + 8)
                o = ps_a[:, 0:(GB + 1) * E_N].rearrange("p (t e) -> p t e", e=E_N)
                mm(o[:, 0:GB, :], tri[:], oh[par][:], start=True, stop=False, skip_group_check=True)
                for t in range(GB):
                    i = mm(o[:, t + 1:GB + 1, :], ones[:], oh[par][:, t:t + 1, :].to_broadcast((P, GB - t, E_N)),
                           start=False, stop=(t == GB - 1), skip_group_check=True)
                i.then_inc(rank_ready, 1)

            pe.wait_ge(w_in, 32)
            ctx_transpose(0, 0)
            project(0, 0)
            project(0, 1)
            x_transpose(0, 0)
            pe.wait_ge(w_rest_in, 48)
            project(0, 2)
            project(0, 3)
            project_v(0)
            ctx_transpose(1, 1)
            project(1, 0)
            project(1, 1)
            x_transpose(1, 1)
            project(1, 2)
            project(1, 3)
            pe.wait_ge(set_by_dve, 5)
            pe.wait_ge(set_by_pool, 5)
            for v in range(LEAD):
                scores(v // UNITS, v // UNITS, v % UNITS)
                if v == UNITS:
                    maxima_transpose(0, 0)

            def step(n, k, grp):
                b, own = k % GB, k // GB
                for u in range(UNITS):
                    m = (u + LEAD) // UNITS
                    if not (known(n) and n + m >= B):
                        scores(n + m, (k + m) % CYCLE, (u + LEAD) % UNITS)
                    if b == 0 and u == 0 and grp(-2) is not None:
                        ranks(grp(-2), own)
                    if b == 0 and u == 2 and grp(1) is not None:
                        project_v(grp(1))
                    if b == 1 and grp(2) is not None:
                        if u == 0:
                            ctx_transpose(grp(2), own)
                        if u == 2:
                            project(grp(2), 0)
                    if b == 2 and grp(2) is not None:
                        if u == 0:
                            project(grp(2), 1)
                        if u == 2:
                            x_transpose(grp(2), own)
                    if b == 3 and u in (0, 2) and grp(2) is not None:
                        project(grp(2), 2 + u // 2)
                    scores_t(n, k, u)
                    if u == 1 and not (known(n) and n == B - 1):
                        maxima_transpose(n + 1, (k + 1) % CYCLE)
                    if u >= 2:
                        weigh_v(n, k, u - 2)
                    elif not (known(n) and n == 0):
                        weigh_v(n - 1, (k - 1) % CYCLE, u + 2)
                    if u == 1 and not (known(n) and n < 2):
                        attn_transpose(n - 2, k % 2)
                    if u == 3 and not (known(n) and n < 2):
                        project_o(n - 2)
                    if u == 3 and not (known(n) and n == 0):
                        o_transpose(n - 1)

            run_steps(pe, step)
            attn_transpose(B - 2, B % 2)
            for u in (2, 3):
                weigh_v(B - 1, CYCLE - 1, u)
            project_o(B - 2)
            ranks(NG - 2, (NG - 2) % 2)
            o_transpose(B - 1)
            attn_transpose(B - 1, CYCLE - 1)
            project_o(B - 1)
            ranks(NG - 1, (NG - 1) % 2)

            def tile_transpose(j, r, lap):
                pe.wait_ge(tile_in[r], lap + 16)
                tr((ps_a[:, 0:P], ps_m[:, 0:P])[r % 2], xt[r][:, D:2 * D], ident[:]).then_inc(xt_T_ready, 1)

            def up(j, r):
                pe.wait_ge(w1_staged, j + 1)
                pe.wait_ge(xt_T_in_sb, j + 1)
                for e in range(2):
                    for c in range(FC):
                        i = mm((ps_s, ps_t)[r % 2][:, e, c * P:(c + 1) * P], w1s[r % 2][:, e, c * P:(c + 1) * P],
                               xtT[r % 2], start=True, stop=True)
                    i.then_inc((h0_ready, h1_ready)[e], 1)

            def down(j, r):
                cls = pe.value_load(tcls_i[0:1, bass.ds(j, 1)], min_val=0, max_val=E_N - 1)
                y = (ps_o, ps_tt)[r % 2][:, 0, :]
                pe.wait_ge(fin_done, j + 1)
                for e in range(2):
                    pe.wait_ge((relu0, relu1)[e], j + 1)
                    for c in range(FC):
                        i = mm(y, hid[r % 2][e][:, c, :], w2[:, bass.ds(cls + e, 1), c, :].rearrange("p e d -> p (e d)"),
                               start=(e == 0 and c == 0), stop=(e == 1 and c == FC - 1))
                i.then_inc(y2_ready, 1)

            pe.sem_inc(y2_ready, 1)
            pe.wait_ge(place_read, NG)
            pe.wait_ge(res_done, B + 1)
            pe.wait_ge(table_ready, 1)
            tile_transpose(0, 0, 0)
            tile_transpose(1, 1, 0)
            up(0, 0)

            def tile(j, r, lap):
                if not (known(j) and j + 1 >= NT):
                    tile_transpose(j + 1, (r + 1) % RING, lap(1))
                up(j, r)
                down(j - 1, (r - 1) % RING)

            run_tiles(pe, tile)
            down(NT - 1, (NT - 1) % RING)

        @block.vector
        def _(dve):
            tt, ts = nc.vector.tensor_tensor, nc.vector.tensor_scalar
            dve.sem_inc(res_done, 1)

            def variances(g, b, st, x_at, op, var_done):
                base = 10 * g
                for t in range(GB):
                    nc.vector.bn_stats(st[:, t, :], x_at(t)).then_inc(op, 1)
                dve.wait_ge(op, base + 4)
                tt(b[:, 0, :], st[:, :, 1], st[:, :, 4], ALU.add).then_inc(op, 1)
                tt(b[:, 1, :], st[:, :, 1], st[:, :, 4], ALU.subtract).then_inc(op, 1)
                tt(b[:, 2, :], st[:, :, 2], st[:, :, 5], ALU.add).then_inc(op, 1)
                dve.wait_ge(op, base + 7)
                ts(b[:, 0, :], b[:, 0, :], -0.5, None, ALU.mult).then_inc(op, 1)
                tt(b[:, 3, :], b[:, 1, :], b[:, 1, :], ALU.mult).then_inc(op, 1)
                ts(b[:, 4, :], b[:, 2, :], 1.0 / D, EPS, ALU.mult, ALU.add).then_inc(op, 1)
                dve.wait_ge(op, base + 10)
                nc.vector.scalar_tensor_tensor(b[:, 5, :], b[:, 3, :], 0.25, b[:, 4, :], ALU.mult,
                                               ALU.add).then_inc(var_done, 1)

            def stats_x(g, par):
                dve.wait_ge(x_in[par], 8 * (g - par) + 16)
                if not (known(g) and g == 0):
                    dve.wait_ge(xn_ready, GB * g)
                variances(g, lnb, stats, lambda t: xin[par][:, t, :], ln_op, var_ready)

            def add_bo(g, par):
                tt(xb[par][:], xin[par][:], bor[:].rearrange("p (b d) -> p b d", b=1).to_broadcast((P, GB, D)),
                   ALU.add).then_inc(xb_ready, 1)

            def route_stats(g, par):
                dve.wait_ge(res_done, GB * (g + 1) + 1)
                variances(g, ln2b, stats2, lambda t: xr[par][:, t, 0:D], ln2_op, var2_ready)

            def route_class(g, par):
                base = 6 * g
                dve.wait_ge(xn2_ready, GB * (g + 1))
                tt(rt[:, :, 95:96], xr[par][:, :, D:D + 1], xr[par][:, :, D + 1:D + 2], ALU.add).then_inc(route_op, 1)
                dve.wait_ge(route_op, base + 1)
                for i, op in enumerate((ALU.is_ge, ALU.is_gt)):
                    tt(rt[:, :, i * NTHR:(i + 1) * NTHR], rt[:, :, 95:96].to_broadcast((P, GB, NTHR)),
                       thr[:, i * NTHR:(i + 1) * NTHR].rearrange("p (b j) -> p b j", b=1).to_broadcast((P, GB, NTHR)),
                       op).then_inc(route_op, 1)
                dve.wait_ge(route_op, base + 3)
                nc.vector.tensor_reduce(rt[:, :, 94], rt[:, :, 0:2 * NTHR], AX.X, ALU.add).then_inc(route_op, 1)
                dve.wait_ge(route_op, base + 4)
                tt(rt[:, :, 40:88], rt[:, :, 94:95].to_broadcast((P, GB, 48)),
                   classes[:].rearrange("p (b j) -> p b j", b=1).to_broadcast((P, GB, 48)),
                   ALU.is_equal).then_inc(route_op, 1)
                dve.wait_ge(route_op, base + 5)
                nc.vector.tensor_reduce(ohf[:], rt[:, :, 40:88].rearrange("p b (e k) -> p b e k", e=E_N), AX.X,
                                        ALU.add).then_inc(route_op, 1)
                dve.wait_ge(route_op, base + 6)
                nc.vector.tensor_copy(oh[par][:], ohf[:]).then_inc(oh_ready, 1)

            def route_place(g, par):
                o = ps_a[:, 0:(GB + 1) * E_N].rearrange("p (t e) -> p t e", e=E_N)
                base = 5 * g
                dve.wait_ge(rank_ready, g + 1)
                old = place[1 - par]
                tt(at[:], o[:, 0:GB, :], old[:].rearrange("p (b e) -> p b e", b=1).to_broadcast((P, GB, E_N)),
                   ALU.add).then_inc(place_op, 1)
                tt(place[par][:], o[:, GB, :], old[:], ALU.add).then_inc(place_read, 1)
                dve.wait_ge(place_op, base + 1)
                tt(at2[:], at[:], ohf[:], ALU.mult).then_inc(place_op, 1)
                dve.wait_ge(place_op, base + 2)
                nc.vector.tensor_reduce(rowf[:], at2[:], AX.X, ALU.add).then_inc(place_op, 1)
                ts(tok[par][:], tok[1 - par][:], float(GT), None, ALU.add).then_inc(place_op, 1)
                dve.wait_ge(place_op, base + 4)
                nc.vector.tensor_copy(xr[par][:, :, 2 * D].bitcast(I32), tok[par][:]).then_inc(place_op, 1)
                dve.wait_ge(place_op, base + 5)
                nc.vector.tensor_copy(rowi[par][:], rowf[:]).then_inc(rowi_ready, 1)

            def rotate(g, i, half):
                dve.wait_ge(proj_ready, 4 * g + 2 * i + half + 1)
                if half == 0 and not (known(g) and g == 0 and i == 0):
                    dve.wait_ge(rot_ready, 2 * g + i)
                dst, tab, done = ((rot1, cosT, cos_done), (rot2, sinT, sin_done))[half]
                nc.vector.scalar_tensor_tensor(dst[:], bank(g, KINDS[2 * i + half]).rearrange("p (b l) -> p b l", b=GB),
                                               bcol[:, 2 * i + half:2 * i + half + 1],
                                               tab[:].rearrange("p (b l) -> p b l", b=1).to_broadcast((P, GB, L)),
                                               ALU.add, ALU.mult).then_inc(done, 1)

            def add_halves(g, i):
                dve.wait_ge(sin_done, 2 * g + i + 1)
                if not (known(g) and g == 0):
                    dve.wait_ge(rest_ready, 2 * g + i - 1)
                tt(rot[i][:], rot1[:].rearrange("p b l -> p (b l)"), rot2[:].rearrange("p b l -> p (b l)"),
                   ALU.add).then_inc(rot_ready, 1)

            def keep_v(g, par):
                dve.wait_ge(vproj_ready, g + 1)
                if not (known(g) and g < 2):
                    dve.wait_ge(pv_done, GB * (g - 1) + 1)
                tt(vaug[par][:, :, :, 0:DH], bank(g, "v").rearrange("p (b h d) -> p b h d", b=GB, h=H),
                   bvr[:].rearrange("p (b h d) -> p b h d", b=1, h=H).to_broadcast((P, GB, H, DH)),
                   ALU.add).then_inc(v_ready, 1)

            def maxima(m, k, u):
                dve.wait_ge(s_ready, UNITS * m + u + 1)
                nc.vector.tensor_reduce(nmax[k % 2][:, u * UH:(u + 1) * UH],
                                        ps_s[:, u % 2, :].rearrange("p (h l) -> p h l", h=UH),
                                        AX.X, ALU.max, negate=True).then_inc(max_done, 1)

            def split_maxima(m, k):
                dve.wait_ge(nmT_ready, m + 1)
                if not (known(m) and m < 2):
                    dve.wait_ge(nm_rows, 32 * (m - 1))
                nc.vector.tensor_copy(nmh[k % 2][:, 0, :], ps_m[0:H, 0:L]).then_inc(nm0_ready, 1)
                dve.wait_ge(nm0_ready, m + 1)
                tt(nmh[k % 2][:, 1, :], ps_m[0:H, 0:L], nmh[k % 2][:, 0, :], ALU.subtract).then_inc(nm_split, 1)

            def normalise(t, k):
                dve.wait_ge(o_ready, t + 1)
                ov = ps_tt[:].rearrange("p u (j w) -> p (u j) w", j=UH)
                nc.vector.reciprocal(rden[k % 2][:], ov[:, :, DH]).then_inc(rden_ready, 1)
                dve.wait_ge(rden_ready, t + 1)
                tt(attn[k % 2][:], ov[:, :, 0:DH],
                   rden[k % 2][:].rearrange("p (h d) -> p h d", d=1).to_broadcast((P, H, DH)),
                   ALU.mult).then_inc(attn_ready, 1)

            def residual(t, k):
                b, par = k % GB, k // GB
                dve.wait_ge(xb_ready, t // GB + 1 if known(t) else (t - b) // GB + 1)
                if b == 0 and not (known(t) and t < CYCLE):
                    dve.wait_ge(rows_out, 16 * (t - GB))
                dve.wait_ge(y_ready, t + 1)
                tt(xr[par][:, b, 0:D], xb[par][:, b, :], ps_m[:, 128:256], ALU.add).then_inc(res_done, 1)

            nc.vector.memset(kst[0][:], 1.0).then_inc(set_by_dve, 1)
            stats_x(0, 0)
            for i in range(2):
                nc.vector.memset(vaug[i][:], 0.0).then_inc(set_by_dve, 1)
            dve.wait_ge(set_by_dve, 3)
            for i in range(2):
                nc.vector.memset(vaug[i][:, :, :, DH:DH + 1], 1.0).then_inc(set_by_dve, 1)
            dve.wait_ge(w_in, 32)
            rotate(0, 0, 0)
            rotate(0, 0, 1)
            add_halves(0, 0)
            stats_x(1, 1)
            rotate(0, 1, 0)
            rotate(0, 1, 1)
            add_halves(0, 1)
            dve.wait_ge(w_rest_in, 48)
            dve.wait_ge(set_by_dve, 5)
            rotate(1, 0, 0)
            rotate(1, 0, 1)
            add_halves(1, 0)
            keep_v(0, 0)
            nc.vector.tensor_copy(place[1][:], place0).then_inc(set_by_dve, 1)
            add_bo(0, 0)
            rotate(1, 1, 0)
            rotate(1, 1, 1)
            add_halves(1, 1)
            dve.wait_ge(set_by_dve, 6)
            for v in range(LEAD):
                maxima(v // UNITS, v // UNITS, v % UNITS)
                if v == UNITS:
                    split_maxima(0, 0)

            def step(n, k, grp):
                b, own = k % GB, k // GB
                for u in range(UNITS):
                    m = (u + LEAD) // UNITS
                    if not (known(n) and n + m >= B):
                        maxima(n + m, (k + m) % CYCLE, (u + LEAD) % UNITS)
                    if u == 0 and not (known(n) and n < 2):
                        normalise(n - 2, k % CYCLE)
                    if u == 1 and not (known(n) and n == B - 1):
                        split_maxima(n + 1, (k + 1) % CYCLE)
                    if b == 0:
                        if u == 0 and grp(-2) is not None:
                            route_place(grp(-2), own)
                        if u == 2 and grp(1) is not None:
                            keep_v(grp(1), 1 - own)
                    if b == 1 and grp(2) is not None:
                        if u == 1:
                            stats_x(grp(2), own)
                        if u == 2:
                            rotate(grp(2), 0, 0)
                    if b == 2:
                        if u == 0 and grp(2) is not None:
                            rotate(grp(2), 0, 1)
                            add_halves(grp(2), 0)
                        if u == 1 and grp(-1) is not None:
                            route_stats(grp(-1), 1 - own)
                    if b == 3:
                        if u in (0, 2) and grp(2) is not None:
                            rotate(grp(2), 1, u // 2)
                        if u == 2 and grp(2) is not None:
                            add_halves(grp(2), 1)
                        if u == 1 and grp(1) is not None:
                            add_bo(grp(1), 1 - own)
                        if u == 1 and grp(-1) is not None:
                            route_class(grp(-1), 1 - own)
                    if u == 3 and not (known(n) and n < 2):
                        residual(n - 2, (k - 2) % CYCLE)

            run_steps(dve, step)
            normalise(B - 2, CYCLE - 2)
            residual(B - 2, CYCLE - 2)
            route_place(NG - 2, (NG - 2) % 2)
            normalise(B - 1, CYCLE - 1)
            residual(B - 1, CYCLE - 1)
            last = (NG - 1) % 2
            route_stats(NG - 1, last)
            route_class(NG - 1, last)
            route_place(NG - 1, last)

            done = [0]

            def link(i):
                done[0] += 1
                i.then_inc(table_op, 1)
                dve.wait_ge(table_op, done[0])

            dve.wait_ge(place_read, NG)
            nc.vector.tensor_copy(padi[:], place[last][:]).then_inc(pad_ready, 1)
            link(tt(cnt[:], place[last][:], place0[:], ALU.subtract))
            v = big_a[:, 0:E_N * 32].rearrange("p (e k) -> p e k", e=E_N)
            link(tt(v, cnt[:].rearrange("p (e k) -> p e k", k=1).to_broadcast((P, E_N, 32)),
                    k128[:].rearrange("p (e k) -> p e k", e=1).to_broadcast((P, E_N, 32)), ALU.is_gt))
            link(nc.vector.tensor_reduce(tiles_of[:], v, AX.X, ALU.add))
            v = big_b[:, 0:E_N * E_N].rearrange("p (e k) -> p e k", e=E_N)
            link(tt(v, lower[:], tiles_of[:].rearrange("p (e k) -> p e k", e=1).to_broadcast((P, E_N, E_N)), ALU.mult))
            link(nc.vector.tensor_reduce(upto[:], v, AX.X, ALU.add))
            v = big_a[:].rearrange("p (j e) -> p j e", e=E_N)
            w = big_b[:].rearrange("p (j e) -> p j e", e=E_N)
            link(tt(v, upto[:].rearrange("p (j e) -> p j e", j=1).to_broadcast((P, NT, E_N)),
                    tile_no[:].rearrange("p (j e) -> p j e", e=1).to_broadcast((P, NT, E_N)), ALU.is_le))
            link(nc.vector.tensor_reduce(tcls[:], v, AX.X, ALU.add))
            link(tt(w, v, tiles_of[:].rearrange("p (j e) -> p j e", j=1).to_broadcast((P, NT, E_N)), ALU.mult))
            link(nc.vector.tensor_reduce(tbef[:], w, AX.X, ALU.add))
            link(tt(tbef[:], tile_no[:], tbef[:], ALU.subtract))
            link(ts(tbef[:], tbef[:], float(P), None, ALU.mult))
            link(nc.vector.scalar_tensor_tensor(trow[:], tcls[:], float(REGION), tbef[:], ALU.mult, ALU.add))
            link(ts(trow[:], trow[:], float(E_N * REGION), None, ALU.min))
            link(ts(tcls[:], tcls[:], float(E_N - 1), None, ALU.min))
            link(nc.vector.tensor_copy(trow_i[:], trow[:]))
            nc.vector.tensor_copy(tcls_i[:], tcls[:]).then_inc(table_ready, 1)
            dve.wait_ge(ffn_in, 16 * (E_N + 4))
            link(tt(b2h[:], b2r[:, 0:E_N, :], b2r[:, 1:E_N + 1, :], ALU.add))
            link(ts(b2h[:], b2h[:], 0.5, None, ALU.mult))

            def stage_w1(j, r, lap):
                cls = dve.value_load(tcls_i[0:1, bass.ds(j, 1)], min_val=0, max_val=E_N - 1)
                if not (known(j) and j < 2):
                    dve.wait_ge(h1_ready, j - 1)
                    dve.wait_ge(relu0, j - 1)
                    dve.wait_ge(relu1, j - 1)
                nc.vector.tensor_copy(w1s[r % 2], w1[:, bass.ds(cls, 2), :]).then_inc(w1_staged, 1)
                dve.wait_ge(tile_in[r], lap + 16)
                tt(xt[r][:, 0:D], xt[r][:, 0:D], b2h[:, bass.ds(cls, 1), :].rearrange("p e d -> p (e d)"),
                   ALU.add).then_inc(b2_added, 1)

            def relu(j, r):
                dve.wait_ge(h1_ready, j + 1)
                dve.wait_ge(w1_staged, j + 1)
                if not (known(j) and j == 0):
                    dve.wait_ge(y2_ready, j)
                for c in range(FC):
                    i = ts(hid[r % 2][1][:, c, :], (ps_s, ps_t)[r % 2][:, 1, c * P:(c + 1) * P],
                           w1s[r % 2][:, 1, DFF + c:DFF + c + 1], 0.0, ALU.add, ALU.max)
                i.then_inc(relu1, 1)

            def finish(j, r):
                dve.wait_ge(b2_added, j + 1)
                dve.wait_ge(y2_ready, j + 2)
                nc.vector.scalar_tensor_tensor(xt[r][:, 0:D], (ps_o, ps_tt)[r % 2][:, 0, :], 0.5, xt[r][:, 0:D],
                                               ALU.mult, ALU.add).then_inc(fin_done, 1)

            dve.sem_inc(fin_done, 2)
            dve.wait_ge(table_ready, 1)
            dve.wait_ge(pv_done, B + 1)
            stage_w1(0, 0, 0)
            stage_w1(1, 1, 0)
            relu(0, 0)

            def tile(j, r, lap):
                if not (known(j) and j + 1 >= NT):
                    stage_w1(j + 1, (r + 1) % RING, lap(1))
                relu(j, r)
                finish(j - 1, (r - 1) % RING)

            run_tiles(dve, tile)
            finish(NT - 1, (NT - 1) % RING)


_INS = ["x", "ctx_1024", "L0_ffn_W1", "L0_ffn_W2"]


def kernel(**inputs):
    import concourse.bacc as bacc
    from concourse.bass_utils import run_bass_kernel_spmd

    nc = bacc.Bacc("TRN2", target_bir_lowering=False, num_devices=1)
    c = np.ascontiguousarray
    arrays = {n: c(inputs[n]) for n in _INS}
    swap = np.arange(D).reshape(D // 2, 2)[:, ::-1].reshape(D)
    w = {n: np.asarray(inputs[f"L0_xattn_W{n}"]) for n in "kqvo"}
    bk, bq, bv, bo = (np.asarray(inputs[f"L0_xattn_b{n}"]) for n in "kqvo")
    again = np.arange(E_N + 1) % E_N
    arrays["b1c"] = c(np.asarray(inputs["L0_ffn_b1"])[again].reshape(E_N + 1, FC, P).transpose(2, 0, 1))
    arrays["b2"] = c(np.asarray(inputs["L0_ffn_b2"])[again][None])
    half = D // 2
    theta = np.float32(1250) ** (-np.arange(half, dtype=np.float32) / np.float32(half))
    ang = np.arange(L, dtype=np.float32)[:, None] * theta
    f32 = np.float32
    cos_t = np.repeat(np.cos(ang), 2, axis=1).T.astype(f32)
    sin_t = np.stack([-np.sin(ang), np.sin(ang)], axis=2).reshape(L, D).T.astype(f32)
    arrays["w_first"] = c(np.stack([np.eye(P, dtype=f32), w["k"].T, w["k"][swap].T, cos_t, sin_t], axis=1))
    arrays["w_rest"] = c(np.stack([w["q"].T, w["q"][swap].T, w["v"].T, w["o"].T], axis=1))
    eye, upper = np.eye(P) * BIG, np.triu(np.ones((P, P)), 1)
    arrays["masks"] = c(np.stack([eye, upper, np.ones((P, P))] + [upper * -BIG] * UH, axis=1).astype(mybir.dt.np(BF16)))
    tok = P * np.arange(GB) - GT + np.arange(P)[:, None]
    pad = np.zeros((P, XW), f32)
    pad[:, 2 * D] = (TOK + np.arange(P, dtype=np.int32)).view(f32)
    arrays["cols"] = c(np.concatenate([np.stack([bk, bk[swap], bq, bq[swap]], axis=1), np.arange(P, dtype=f32)[:, None],
                                       tok.astype(f32), pad], axis=1))
    j = np.arange(1, NTHR + 1)
    shared = [j, -j, NTHR + np.arange(E_N)[:, None] + 8 * (np.arange(6) - 3), np.arange(E_N) * REGION,
              np.arange(32) * P, np.arange(NT), np.tril(np.ones((E_N, E_N)))]
    arrays["row_consts"] = np.concatenate([bv, bo] + [v.reshape(-1).astype(f32) for v in shared])[None, :]
    aps = {n: nc.dram_tensor(f"in_{n}", v.shape, mybir.dt.from_np(v.dtype), kind="ExternalInput").ap()
           for n, v in arrays.items()}
    out = nc.dram_tensor("out_0", (B, L, D), F32, kind="ExternalOutput").ap()
    build(nc, aps, out)
    r = run_bass_kernel_spmd(nc, [{f"in_{n}": v for n, v in arrays.items()}], core_ids=[0])
    return r.results[0]["out_0"]
```
